# Optimizing a Trainium2 kernel written in Bass

```python
import numpy as np
import jax
import jax.numpy as jnp

def _softmax(x, axis=-1):
    return jax.nn.softmax(x, axis=axis)

def _gelu(x):
    return jax.nn.gelu(x, approximate=True)

def _silu(x):
    return jax.nn.silu(x)

def _sigmoid(x):
    return jax.nn.sigmoid(x)

def _layernorm(x, axis=-1, eps=1e-05):
    m = jnp.mean(x, axis=axis, keepdims=True)
    v = jnp.var(x, axis=axis, keepdims=True)
    return (x - m) / jnp.sqrt(v + eps)

def _scatter_add(tgt, idx, src, axis=0):
    return tgt.at[idx].add(src)

def _segment_sum(src, seg, n):
    return jax.ops.segment_sum(src, seg, n)
kernel_name = 'mk_adaln_attn_ffn_d1_seqx_r4_bd2cd5'

def setup_inputs(seed: int=0):
    np.random.seed(seed)
    _w = jnp.asarray

    def _rec_inputs():
        import jax
        import jax.numpy as jnp
        _rk = jax.random.key(seed)
        x = -7.109e-05 + 0.9999 * jax.random.normal(jax.random.fold_in(_rk, 1), (16, 256, 256), jnp.float32)
        _lenS = 256 - jax.random.randint(jax.random.fold_in(_rk, 7), (16,), 0, max(1, 256 // 4) + 1, jnp.int32)
        _lenS2 = 256 - jax.random.randint(jax.random.fold_in(_rk, 8), (16,), 0, max(1, 256 // 4) + 1, jnp.int32)
        itok_B_0_8 = jax.random.randint(jax.random.fold_in(_rk, 11), (16,), 0, 9, jnp.int32)
        itok_B_0_15 = jax.random.randint(jax.random.fold_in(_rk, 12), (16,), 0, 16, jnp.int32)
        return (x, itok_B_0_8, itok_B_0_15)
    x, itok_B_0_8, itok_B_0_15 = _rec_inputs()

    def _L0_cond_setup():
        import jax, jax.numpy as jnp
        import numpy as np
        LN_EPS = 1e-05
        key = jax.random.key(seed)
        ks = jax.random.split(key, 8)
        B, S, H, A, L = (32, 512, 256, 64, 10)
        return {'hidden_states': jax.random.normal(ks[0], (B, S, H), dtype=jnp.float32), 'language_ids': jax.random.randint(ks[1], (B,), 0, L, dtype=jnp.int64), 'W1': jax.random.normal(ks[2], (L, H, A), dtype=jnp.float32) * (1.0 / np.sqrt(H)), 'b1': jnp.zeros((L, A), dtype=jnp.float32), 'W2': jax.random.normal(ks[3], (L, A, H), dtype=jnp.float32) * (1.0 / np.sqrt(A)), 'b2': jnp.zeros((L, H), dtype=jnp.float32), 'gamma': jnp.ones((L, H), dtype=jnp.float32), 'beta': jnp.zeros((L, H), dtype=jnp.float32)}
    _L0_cond_all = _L0_cond_setup()
    _L0_cond_in = {k: v for k, v in _L0_cond_all.items() if k in ('W1', 'b1', 'W2', 'b2', 'gamma', 'beta')}
    del _L0_cond_all

    def _L0_attn_setup():
        import jax, jax.numpy as jnp
        import numpy as np
        import math
        B, T, WIDTH, NUM_HEADS, WINDOW = (2, 512, 256, 16, 256)
        HEAD_DIM = WIDTH // NUM_HEADS
        _MIN_LOGITS_VALUE = -1e+30
        key = jax.random.key(seed)
        k1, k2, k3, k4, k5 = jax.random.split(key, 5)
        std = math.sqrt(1.0 / WIDTH)
        x = jax.random.normal(k1, (B, T, WIDTH), dtype=jnp.float32)
        segment_pos = jnp.tile(jnp.arange(T, dtype=jnp.int32)[None, :], (B, 1))
        Wq = jax.random.normal(k2, (WIDTH, WIDTH), dtype=jnp.float32) * std
        Wk = jax.random.normal(k3, (HEAD_DIM, WIDTH), dtype=jnp.float32) * std
        Wv = jax.random.normal(k4, (HEAD_DIM, WIDTH), dtype=jnp.float32) * std
        Wf = jax.random.normal(k5, (WIDTH, WIDTH), dtype=jnp.float32) * std
        bf = jnp.zeros((WIDTH,), dtype=jnp.float32)
        return {'x': x, 'segment_pos': segment_pos, 'Wq': Wq, 'Wk': Wk, 'Wv': Wv, 'Wf': Wf, 'bf': bf}
    _L0_attn_all = _L0_attn_setup()
    _L0_attn_in = {k: v for k, v in _L0_attn_all.items() if k in ('segment_pos', 'Wq', 'Wk', 'Wv', 'Wf', 'bf')}
    del _L0_attn_all

    def _L0_cond2_setup():
        import jax, jax.numpy as jnp
        import numpy as np
        B, N, DIM = (32, 256, 256)
        HID = 1024
        PART = 64
        OUT = 256
        SHARED = OUT - PART
        E = 16
        key = jax.random.key(seed)
        ks = jax.random.split(key, 8)
        s = 0.02
        return {'x': jax.random.normal(ks[0], (B, N, DIM), dtype=jnp.float32), 'indices': jax.random.randint(ks[1], (B,), 0, E, dtype=jnp.int64), 'fc1_w': jax.random.normal(ks[2], (HID, DIM), dtype=jnp.float32) * s, 'fc1_b': jnp.zeros((HID,), dtype=jnp.float32), 'fc2_w': jax.random.normal(ks[3], (SHARED, HID), dtype=jnp.float32) * s, 'fc2_b': jnp.zeros((SHARED,), dtype=jnp.float32), 'experts_w': jax.random.normal(ks[4], (E, PART, HID), dtype=jnp.float32) * s, 'experts_b': jnp.zeros((E, PART), dtype=jnp.float32)}
    _L0_cond2_all = _L0_cond2_setup()
    _L0_cond2_in = {k: v for k, v in _L0_cond2_all.items() if k in ('fc1_w', 'fc1_b', 'fc2_w', 'fc2_b', 'experts_w', 'experts_b')}
    del _L0_cond2_all

    def _L0_ffn_setup():
        import jax, jax.numpy as jnp
        import numpy as np
        D_IN, D_HID = (256, 1024)

        def _ternary(key, shape):
            return jax.random.randint(key, shape, -1, 2).astype(jnp.float32)

        def _tlin(x, w, s):
            return jnp.einsum('bsi,oi->bso', x, w) * s
        key = jax.random.key(seed)
        ks = jax.random.split(key, 12)
        inv = lambda fan: 1.0 / np.sqrt(fan).astype(np.float32)
        return {'x': jax.random.normal(ks[0], (4, 512, D_IN), dtype=jnp.float32), 'w1_w': _ternary(ks[1], (D_HID, D_IN)), 'w1_s': jax.random.uniform(ks[2], (D_HID,), dtype=jnp.float32) * inv(D_IN), 'w2_w': _ternary(ks[3], (D_HID, D_IN)), 'w2_s': jax.random.uniform(ks[4], (D_HID,), dtype=jnp.float32) * inv(D_IN), 'h1_w': _ternary(ks[5], (D_HID, D_HID)), 'h1_s': jax.random.uniform(ks[6], (D_HID,), dtype=jnp.float32) * inv(D_HID), 'h2_w': _ternary(ks[7], (D_HID, D_HID)), 'h2_s': jax.random.uniform(ks[8], (D_HID,), dtype=jnp.float32) * inv(D_HID), 'w3_w': _ternary(ks[9], (D_IN, D_HID)), 'w3_s': jax.random.uniform(ks[10], (D_IN,), dtype=jnp.float32) * inv(D_HID)}
    _L0_ffn_all = _L0_ffn_setup()
    _L0_ffn_in = {k: v for k, v in _L0_ffn_all.items() if k in ('w1_w', 'w1_s', 'w2_w', 'w2_s', 'h1_w', 'h1_s', 'h2_w', 'h2_s', 'w3_w', 'w3_s')}
    del _L0_ffn_all
    return {'x': x, 'itok_B_0_8': itok_B_0_8, 'itok_B_0_15': itok_B_0_15, 'L0_cond_W1': _L0_cond_in['W1'], 'L0_cond_b1': _L0_cond_in['b1'], 'L0_cond_W2': _L0_cond_in['W2'], 'L0_cond_b2': _L0_cond_in['b2'], 'L0_cond_gamma': _L0_cond_in['gamma'], 'L0_cond_beta': _L0_cond_in['beta'], 'L0_attn_segment_pos': _L0_attn_in['segment_pos'], 'L0_attn_Wq': _L0_attn_in['Wq'], 'L0_attn_Wk': _L0_attn_in['Wk'], 'L0_attn_Wv': _L0_attn_in['Wv'], 'L0_attn_Wf': _L0_attn_in['Wf'], 'L0_attn_bf': _L0_attn_in['bf'], 'L0_cond2_fc1_w': _L0_cond2_in['fc1_w'], 'L0_cond2_fc1_b': _L0_cond2_in['fc1_b'], 'L0_cond2_fc2_w': _L0_cond2_in['fc2_w'], 'L0_cond2_fc2_b': _L0_cond2_in['fc2_b'], 'L0_cond2_experts_w': _L0_cond2_in['experts_w'], 'L0_cond2_experts_b': _L0_cond2_in['experts_b'], 'L0_ffn_w1_w': _L0_ffn_in['w1_w'], 'L0_ffn_w1_s': _L0_ffn_in['w1_s'], 'L0_ffn_w2_w': _L0_ffn_in['w2_w'], 'L0_ffn_w2_s': _L0_ffn_in['w2_s'], 'L0_ffn_h1_w': _L0_ffn_in['h1_w'], 'L0_ffn_h1_s': _L0_ffn_in['h1_s'], 'L0_ffn_h2_w': _L0_ffn_in['h2_w'], 'L0_ffn_h2_s': _L0_ffn_in['h2_s'], 'L0_ffn_w3_w': _L0_ffn_in['w3_w'], 'L0_ffn_w3_s': _L0_ffn_in['w3_s']}

def reference(x, itok_B_0_8, itok_B_0_15, L0_cond_W1, L0_cond_b1, L0_cond_W2, L0_cond_b2, L0_cond_gamma, L0_cond_beta, L0_attn_segment_pos, L0_attn_Wq, L0_attn_Wk, L0_attn_Wv, L0_attn_Wf, L0_attn_bf, L0_cond2_fc1_w, L0_cond2_fc1_b, L0_cond2_fc2_w, L0_cond2_fc2_b, L0_cond2_experts_w, L0_cond2_experts_b, L0_ffn_w1_w, L0_ffn_w1_s, L0_ffn_w2_w, L0_ffn_w2_s, L0_ffn_h1_w, L0_ffn_h1_s, L0_ffn_h2_w, L0_ffn_h2_s, L0_ffn_w3_w, L0_ffn_w3_s):
    import jax
    import jax.numpy as jnp

    def _L0_cond_ref(hidden_states, language_ids, W1, b1, W2, b2, gamma, beta):
        import jax, jax.numpy as jnp
        import numpy as np
        LN_EPS = 1e-05
        w1 = W1[language_ids]
        w2 = W2[language_ids]
        h = jnp.einsum('bsh,bha->bsa', hidden_states, w1) + b1[language_ids][:, None, :]
        h = jax.nn.relu(h)
        adapted = jnp.einsum('bsa,bah->bsh', h, w2) + b2[language_ids][:, None, :]
        x = hidden_states + adapted
        mean = jnp.mean(x, axis=-1, keepdims=True)
        var = jnp.mean(jnp.square(x - mean), axis=-1, keepdims=True)
        normed = (x - mean) * jax.lax.rsqrt(var + LN_EPS)
        return normed * gamma[language_ids][:, None, :] + beta[language_ids][:, None, :]

    def _L0_attn_ref(x, segment_pos, Wq, Wk, Wv, Wf, bf):
        import jax, jax.numpy as jnp
        import numpy as np
        import math
        B, T, WIDTH, NUM_HEADS, WINDOW = (2, 512, 256, 16, 256)
        HEAD_DIM = WIDTH // NUM_HEADS
        _MIN_LOGITS_VALUE = -1e+30
        b, t, _ = x.shape
        q = (x @ Wq.T).reshape(b, t, NUM_HEADS, HEAD_DIM)
        k = x @ Wk.T
        v = x @ Wv.T
        scale = 1.0 / math.sqrt(HEAD_DIM)
        logits = jnp.einsum('btnh,bsh->bnts', q, k) * scale
        pos = jnp.arange(t)
        q_pos = pos[:, None]
        k_pos = pos[None, :]
        mask = (q_pos >= k_pos) & (q_pos <= k_pos + WINDOW)
        masked = jnp.where(mask[None, None, :, :], logits, _MIN_LOGITS_VALUE)
        probs = jax.nn.softmax(masked.astype(jnp.float32), axis=-1).astype(logits.dtype)
        out = jnp.einsum('bnts,bsh->btnh', probs, v).reshape(b, t, WIDTH)
        return out @ Wf.T + bf

    def _L0_cond2_ref(x, indices, fc1_w, fc1_b, fc2_w, fc2_b, experts_w, experts_b):
        import jax, jax.numpy as jnp
        import numpy as np
        B, N, DIM = (32, 256, 256)
        HID = 1024
        PART = 64
        OUT = 256
        SHARED = OUT - PART
        E = 16
        h = jax.nn.gelu(jnp.einsum('bnd,hd->bnh', x, fc1_w) + fc1_b, approximate=False)
        shared = jnp.einsum('bnh,sh->bns', h, fc2_w) + fc2_b
        We = experts_w[indices]
        be = experts_b[indices]
        expert_x = jnp.einsum('bnh,bph->bnp', h, We) + be[:, None, :]
        return jnp.concatenate([shared, expert_x], axis=-1)

    def _L0_ffn_ref(x, w1_w, w1_s, w2_w, w2_s, h1_w, h1_s, h2_w, h2_s, w3_w, w3_s):
        import jax, jax.numpy as jnp
        import numpy as np
        D_IN, D_HID = (256, 1024)

        def _ternary(key, shape):
            return jax.random.randint(key, shape, -1, 2).astype(jnp.float32)

        def _tlin(x, w, s):
            return jnp.einsum('bsi,oi->bso', x, w) * s
        h = jax.nn.silu(_tlin(x, w1_w, w1_s)) * _tlin(x, w2_w, w2_s)
        h = jax.nn.gelu(_tlin(h, h1_w, h1_s), approximate=False)
        h = jax.nn.gelu(_tlin(h, h2_w, h2_s), approximate=False)
        return _tlin(h, w3_w, w3_s)
    x = x + _L0_attn_ref(_L0_cond_ref(x, itok_B_0_8, L0_cond_W1, L0_cond_b1, L0_cond_W2, L0_cond_b2, L0_cond_gamma, L0_cond_beta), L0_attn_segment_pos, L0_attn_Wq, L0_attn_Wk, L0_attn_Wv, L0_attn_Wf, L0_attn_bf)
    x = x + _L0_ffn_ref(_L0_cond2_ref(x, itok_B_0_15, L0_cond2_fc1_w, L0_cond2_fc1_b, L0_cond2_fc2_w, L0_cond2_fc2_b, L0_cond2_experts_w, L0_cond2_experts_b), L0_ffn_w1_w, L0_ffn_w1_s, L0_ffn_w2_w, L0_ffn_w2_s, L0_ffn_h1_w, L0_ffn_h1_s, L0_ffn_h2_w, L0_ffn_h2_s, L0_ffn_w3_w, L0_ffn_w3_s)
    return x

_drawn_inputs = setup_inputs


def setup_inputs(seed=0):
    import zlib

    import numpy as np

    out = dict(_drawn_inputs(seed))
    spreads = {'L0_cond_b1': (0.0, 0.1),
     'L0_cond_b2': (0.0, 0.1),
     'L0_cond_gamma': (1.0, 0.2),
     'L0_cond_beta': (0.0, 0.1),
     'L0_attn_bf': (0.0, 0.1),
     'L0_cond2_fc1_b': (0.0, 0.1),
     'L0_cond2_fc2_b': (0.0, 0.1),
     'L0_cond2_experts_b': (0.0, 0.1)}
    factors = {}
    for name, (base, spread) in spreads.items():
        noise = np.random.default_rng([zlib.crc32(name.encode()), seed]).standard_normal(out[name].shape)
        drawn = base * np.exp(spread * noise) if base else spread * noise
        out[name] = jnp.asarray(drawn.astype(out[name].dtype))
    for name, factor in factors.items():
        out[name] = (out[name] * factor).astype(out[name].dtype)
    return out
```

```python
from contextlib import ExitStack

import numpy as np

import concourse.bass as bass
from concourse import mybir

F32 = mybir.dt.float32
F32R = mybir.dt.float32r
BF16 = mybir.dt.bfloat16
I32 = mybir.dt.int32
U32 = mybir.dt.uint32
ALU = mybir.AluOpType
ACT = mybir.ActivationFunctionType
AX = mybir.AxisListType

P = 128
B, T, D = 16, 256, 256
KD = D // P
NT = T // P
TOK = B * T
L, A = 10, 64
NH, HD = 16, 16
NP = NH // 2
SLOT = 64
HID = 1024
KH = HID // P
E, PART = 16, 64
SHARED = D - PART
EPS = 1e-5
HEAD = 1
HEAD_STARTED = """xa_split expert_split y_ready yc_split out_ready score_mm ring_mm unit_mm act_ready prod_ready
    keys_moved values_moved x1_stored y_stored c_act out_stored ring_dve exp_done front_act front_dve ring_act""".split()
C_UNITS = 4 * KH + KD
QSCALE = HD ** -0.5

TW = 512
TILES = TOK // TW
BT = TW // T

W1_AT = 0
W2_AT = W1_AT + KD * HID
H1_AT = W2_AT + KD * HID
H2_AT = H1_AT + KH * HID
W3_AT = H2_AT + KH * HID
FFN_COLS = W3_AT + KH * D
CHECK = FFN_COLS // TILES

RING = (["act", "dve"] * 2
        + ["dve"] * 12
        + ["act"]
        + ["dve", "dve"]
        + ["act"]
        + ["dve", "dve"])
FRONT = ["act", "dve", "act", "dve", "dve", "dve"]


def emptied(order, j):
    return order[j], order[:j + 1].count(order[j])


def max_fill(j):
    f = j - 4
    if f < 4:
        return 0, f % 2, 4 * (f // 2), 4
    f -= 4
    return 1, f % 2, 2 * (f // 2), 2


def build(nc, x_t, x_tok, lang, expert, cond_w1, cond_w2, cond_vec, w_qv, w_k, w_f, b_f, ident_d, mask_d, sel_d,
          fc1_w, fc1_b, fc2_w, fc2_b, exp_w, exp_b, ffn_d, ffn_s, out_t):
    ctx = ExitStack()
    with ctx:
        def sb(name, shape, dt=F32, where=ctx):
            return where.enter_context(nc.sbuf_tensor(name, shape, dt))

        def sem(name):
            return ctx.enter_context(nc.semaphore(name))

        bank = [ctx.enter_context(nc.psum_tensor(f"bank{i}", [P, 512], F32)) for i in range(4)]
        score_bank = [ctx.enter_context(nc.psum_tensor(f"score{i}", [P, 2, 512], F32)) for i in range(2)]
        ring = bank[0:2]
        front = bank[2:4]

        ffn_scratch = nc.dram_tensor("ffn_scratch", (P, FFN_COLS), F32).ap()
        x1_scratch = nc.dram_tensor("x1_scratch", (P, KD, TOK), F32).ap()
        y_scratch = nc.dram_tensor("y_scratch", (P, KD, TOK), F32).ap()

        ffn_w = sb("ffn_w", [P, FFN_COLS], F32R)
        fc1_bias = sb("fc1_bias", [P, KH])
        fc2_bias = sb("fc2_bias", [P, 1 + BT])
        scales = sb("scales", [P, 4 * KH + KD])
        low_bits = sb("low_bits", [P, 1])
        low_count = sb("low_count", [1, 1], I32)
        ones = sb("ones", [P, 1])
        SC_W1, SC_W2, SC_H1, SC_H2 = (scales[:, i * KH:(i + 1) * KH] for i in range(4))

        SC_W3 = scales[:, 4 * KH:4 * KH + KD]

        s = {}
        for name in """
                sp_settled pool_settled dve_settled raw_loaded const_loaded sel_loaded ffn_copied ffn_loaded fc_split split_step const_made sel_made row_made
                front_loaded front_mm front_act front_dve
                stats_ready moments_ready veps_ready rstd_ready norm_ready
                keys_hi keys_low q_hi q_low q_again keys_moved values_moved
                ring_mm ring_act ring_dve minus_max m2_hi m2_ready
                score_mm exp_done masked recip_done resid_loaded x1_stored
                phase1_over phase2_over
                xa_loaded xa_hi xa_split expert_loaded expert_hi expert_split bias_loaded
                unit_mm unit_act unit_dve raw_ready hi_ready act_ready y_hi y_ready y_stored
                bits_step bits_max bits_summed flag_ready
                yc_loaded yc_hi yc_split resid2_loaded sil_ready prod_ready c_mm c_act c_dve c_raw c_hi c_ready
                out_ready out_stored""".split():
            s[name] = sem(name)

        early = ExitStack()
        fc1_hi = sb("fc1_hi", [P, KD, HID], F32R, early)
        fc1_lo = sb("fc1_lo", [P, KD, HID], F32R, early)
        fc2a_hi = sb("fc2a_hi", [P, KH, P], F32R, early)
        fc2a_lo = sb("fc2a_lo", [P, KH, P], F32R, early)
        fc2b_hi = sb("fc2b_hi", [P, KH, BT, P], F32R, early)
        fc2b_lo = sb("fc2b_lo", [P, KH, BT, P], F32R, early)

        one = ExitStack()
        xt = sb("xt", [P, KD, T], F32, one)
        xtok = sb("xtok", [P, NT, D], F32, one)
        w1c = sb("w1c", [P, KD, A], F32, one)
        w2c = sb("w2c", [A + 1, D], F32, one)
        vec = sb("vec", [P, 5], F32, one)
        wqv = sb("wqv", [P, KD, D + HD], F32, one)
        wk = sb("wk", [P, KD, P], F32, one)
        wf = sb("wf", [P, KD, D], F32, one)
        bf = sb("bf", [P, KD], F32, one)
        ident = sb("ident", [P, P], F32, one)
        ident_b = sb("ident_b", [P, P], BF16, one)
        mask = sb("mask", [P, 4, P], BF16, one)
        sel = sb("sel", [P, NH, P], F32R, one)
        h_t = sb("h_t", [A + 1, T], F32, one)
        u = sb("u", [P, NT, D], F32, one)
        stats = sb("stats", [P, NT, 6], F32, one)
        moments = sb("moments", [P, NT, 2], F32, one)
        veps = sb("veps", [P, NT], F32, one)
        half = sb("half", [P, NT], F32, one)
        rstd = sb("rstd", [P, NT], F32, one)
        norm = sb("norm", [P, NT, D], F32, one)
        norm_t = sb("norm_t", [P, KD, T], F32, one)
        q_parts = sb("q_parts", [P, NT, NH, SLOT], F32, one)
        q_t = sb("q_t", [P, NP, T], F32R, one)
        keys_new = sb("keys_new", [P, T], F32R, one)
        keys = sb("keys", [P, T], F32R, one)
        values_new = sb("values_new", [P, NT, HD + 1], F32, one)
        values = sb("values", [P, NT, HD + 1], F32, one)
        neg_max = sb("neg_max", [P, NT, NP, 2], F32, one)
        m2 = sb("m2", [P, NT, 2, SLOT], F32, one)
        m_t = sb("m_t", [P, T], F32R, one)
        p0 = sb("p0", [P, 4, 2, 2, T], F32, one)
        p1 = sb("p1", [P, 2, 2, 4, P], F32, one)
        p0_flat = p0[:, :, :, :, :].rearrange("p a b c t -> p (a b c t)")
        fc1_raw = p0_flat[:, 0:KD * HID]
        fc2_raw = p0_flat[:, KD * HID:KD * HID + KH * SHARED].rearrange("p (k o) -> p k o", k=KH)
        sel_raw = p1[:, :, :, :, :].rearrange("p a b c t -> p (a b c t)")
        recip = sb("recip", [P, NT, NH], F32, one)
        att = norm
        att_t = sb("att_t", [P, KD, T], F32, one)
        resid = sb("resid", [P, KD, T], F32, one)
        x1 = sb("x1", [P, KD, T], F32, one)
        one.close()

        two = ExitStack()
        xa = sb("xa", [P, KD, TW], F32, two)
        xa_hi = sb("xa_hi_b", [P, KD, TW], F32R, two)
        xa_lo = sb("xa_lo_b", [P, KD, TW], F32R, two)
        exp_raw = sb("exp_raw", [P, BT, KH, PART], F32, two)
        g_hi = sb("g_hi", [P, KH, TW], F32R, two)
        g_lo = sb("g_lo", [P, KH, TW], F32R, two)
        g_raw = sb("g_raw", [P, 2, TW], F32, two)
        y = sb("y", [P, KD, TW], F32, two)
        bits = sb("bits", [P, CHECK], U32, two)
        bits_low = sb("bits_low", [P, CHECK], U32, two)
        bits_top = sb("bits_top", [P, 1], U32, two)
        two.close()
        early.close()

        three = ExitStack()
        yc = sb("yc", [P, KD, TW], F32, three)
        yc_hi = sb("yc_hi_b", [P, KD, TW], F32R, three)
        yc_lo = sb("yc_lo_b", [P, KD, TW], F32R, three)
        h_hi = [sb(f"h{i}_hi", [P, KH, TW], F32R, three) for i in range(2)]
        h_lo = [sb(f"h{i}_lo", [P, KH, TW], F32R, three) for i in range(2)]
        sil = sb("sil", [P, 2, TW], F32, three)
        h_raw = sb("h_raw", [P, 2, TW], F32, three)
        resid2 = sb("resid2", [P, KD, TW], F32, three)
        outs = sb("outs", [P, KD, TW], F32, three)
        three.close()

        block = ctx.enter_context(nc.Block())

        def fill_at(b, order, j):
            return b * len(order) + j + 1

        def wait_emptied(eng, order, act_sem, dve_sem, b, j):
            who, n = emptied(order, j)
            eng.wait_ge(act_sem if who == "act" else dve_sem, HEAD + b * order.count(who) + n)

        def settle(eng, name):
            eng.sem_inc(s[name], 1)

        @block.sync
        def _(sp):
            def load_front(n):
                if True:
                    l = sp.value_load(lang[0:1, bass.ds(n, 1)], min_val=0, max_val=L - 1)
                    if not (isinstance(n, int) and n == 0):
                        sp.wait_ge(s["front_mm"], (n - 1) * len(FRONT) + 2)
                    sp.dma_start(xt[:, :, :], x_t[:, :, bass.ds(n * T, T)]).then_inc(s["front_loaded"], 16)
                    sp.dma_start(w1c[:, :, :], cond_w1[bass.ds(l, 1)].rearrange("a p k h -> p (a k) h")).then_inc(s["front_loaded"], 16)
                    sp.dma_start(w2c[:, :], cond_w2[bass.ds(l, 1)].rearrange("a p h -> p (a h)")).then_inc(s["front_loaded"], 16)
                    if not (isinstance(n, int) and n == 0):
                        sp.wait_ge(s["front_dve"], HEAD + 4 * (n - 1) + 1)
                        settle(sp, "sp_settled")
                        sp.wait_ge(s["front_act"], HEAD + 2 * n)
                        settle(sp, "sp_settled")
                    sp.dma_start(xtok[:, :, :], x_tok[bass.ds(n, 1)].rearrange("a p t d -> p (a t) d")).then_inc(s["front_loaded"], 16)
                    sp.dma_start(vec[:, :], cond_vec[bass.ds(l, 1)].rearrange("a p c -> p (a c)")).then_inc(s["front_loaded"], 16)

            def load_resid(b):
                if not (isinstance(b, int) and b == 0):
                    sp.wait_ge(s["ring_dve"], HEAD + b * RING.count("dve"))
                sp.dma_start(resid[:, :, :], x_t[:, :, bass.ds(b * T, T)]).then_inc(s["resid_loaded"], 16)

            def store_x1(b):
                sp.wait_ge(s["ring_dve"], HEAD + (b + 1) * RING.count("dve"))
                sp.dma_start(x1_scratch[:, :, bass.ds(b * T, T)], x1[:, :, :]).then_inc(s["x1_stored"], 16)

            load_front(0)
            sp.dma_start(ident[:, :], ident_d).then_inc(s["const_loaded"], 16)
            sp.dma_start(wqv[:, :, :], w_qv).then_inc(s["const_loaded"], 16)
            sp.dma_start(wk[:, :, :], w_k).then_inc(s["const_loaded"], 16)
            sp.dma_start(wf[:, :, :], w_f).then_inc(s["const_loaded"], 16)
            sp.dma_start(bf[:, :], b_f).then_inc(s["const_loaded"], 16)
            sp.dma_start(mask[:, :, :], mask_d).then_inc(s["const_loaded"], 16)
            sp.dma_start(sel_raw, sel_d).then_inc(s["sel_loaded"], 16)
            load_resid(0)
            sp.dma_start(fc1_raw, fc1_w).then_inc(s["raw_loaded"], 16)
            sp.dma_start(fc2_raw, fc2_w).then_inc(s["raw_loaded"], 16)
            sp.dma_start(fc1_bias[:, :], fc1_b).then_inc(s["raw_loaded"], 16)
            sp.dma_start(scales[:, :], ffn_s).then_inc(s["raw_loaded"], 16)
            load_front(1)
            sp.dma_start(ffn_scratch, ffn_d).then_inc(s["ffn_copied"], 16)
            sp.wait_ge(s["ffn_copied"], 16)
            sp.dma_start(ffn_w[:, :].bitcast(F32), ffn_scratch).then_inc(s["ffn_loaded"], 16)
            with sp.Fori(0, B - 2) as b:
                load_front(b + 2)
                store_x1(b)
                load_resid(b + 1)
            store_x1(B - 2)
            load_resid(B - 1)
            store_x1(B - 1)
            sp.wait_ge(s["x1_stored"], HEAD + 16 * B)
            sp.wait_ge(s["phase1_over"], 4)

            def load_expert(t):
                for j in range(BT):
                    e = sp.value_load(expert[0:1, bass.ds(t * BT + j, 1)], min_val=0, max_val=E - 1)
                    sp.dma_start(exp_raw[:, j], exp_w[bass.ds(e, 1)].rearrange("a p k h -> p (a k) h")).then_inc(s["expert_loaded"], 16)
                    sp.dma_start(fc2_bias[SHARED - P:P, 1 + j:2 + j], exp_b[bass.ds(e, 1)].rearrange("a p o -> p (a o)")).then_inc(s["bias_loaded"], 16)

            sp.dma_start(fc2_bias[:, 0:1], fc2_b[0]).then_inc(s["bias_loaded"], 16)
            for j in range(BT):
                sp.dma_start(fc2_bias[0:SHARED - P, 1 + j:2 + j], fc2_b[1, 0:SHARED - P]).then_inc(s["bias_loaded"], 16)

            with sp.Fori(0, TILES) as t:
                sp.wait_ge(s["xa_split"], HEAD + t)
                sp.dma_start(xa[:, :, :], x1_scratch[:, :, bass.ds(t * TW, TW)]).then_inc(s["xa_loaded"], 16)
                sp.wait_ge(s["expert_split"], HEAD + 2 * t)
                settle(sp, "sp_settled")
                sp.wait_ge(s["y_ready"], HEAD + 3 * t)
                settle(sp, "sp_settled")
                load_expert(t)
                sp.wait_ge(s["y_ready"], HEAD + 3 * (t + 1))
                sp.dma_start(y_scratch[:, :, bass.ds(t * TW, TW)], y[:, :, :]).then_inc(s["y_stored"], 16)
            sp.wait_ge(s["y_stored"], HEAD + 16 * TILES)
            sp.wait_ge(s["phase2_over"], 4)

            with sp.Fori(0, TILES) as t:
                sp.wait_ge(s["yc_split"], HEAD + t)
                sp.dma_start(yc[:, :, :], y_scratch[:, :, bass.ds(t * TW, TW)]).then_inc(s["yc_loaded"], 16)
                sp.wait_ge(s["out_ready"], HEAD + KD * t)
                sp.dma_start(resid2[:, :, :], x1_scratch[:, :, bass.ds(t * TW, TW)]).then_inc(s["resid2_loaded"], 16)
                sp.wait_ge(s["out_ready"], HEAD + KD * (t + 1))
                sp.dma_start(out_t[:, :, bass.ds(t * TW, TW)], outs[:, :, :]).then_inc(s["out_stored"], 16)
            sp.wait_ge(s["out_stored"], HEAD + 16 * TILES)

        @block.gpsimd
        def _(pool):
            for name in HEAD_STARTED:
                pool.sem_inc(s[name], HEAD)
            nc.gpsimd.memset(q_parts[:, :, :, :], 0.0).then_inc(s["const_made"], 1)
            nc.gpsimd.memset(m2[:, :, :, :], 0.0).then_inc(s["const_made"], 1)
            nc.gpsimd.memset(half[:, :], -0.5).then_inc(s["const_made"], 1)
            nc.gpsimd.memset(values_new[:, :, HD:HD + 1], 1.0).then_inc(s["const_made"], 1)
            nc.gpsimd.memset(ones[:, :], 1.0).then_inc(s["const_made"], 1)
            pool.wait_ge(s["sel_loaded"], 16)
            nc.gpsimd.tensor_copy(sel[:, :, :], sel_raw.rearrange("p (h m) -> p h m", h=NH)).then_inc(s["sel_made"], 1)
            pool.wait_ge(s["const_loaded"], 96)
            nc.gpsimd.tensor_copy(ident_b[:, :], ident[:, :]).then_inc(s["sel_made"], 1)

            def rstd_of(n):
                pool.wait_ge(s["veps_ready"], n + 1)
                if isinstance(n, int) and n == 0:
                    pool.wait_ge(s["const_made"], 5)
                nc.gpsimd.tensor_tensor(rstd[:, :], veps[:, :], half[:, :], ALU.pow).then_inc(s["rstd_ready"], 1)

            def high_again(n):
                for t in range(NT):
                    pool.wait_ge(s["q_hi"], NT * n + t + 1)
                    settle(pool, "pool_settled")
                    nc.gpsimd.tensor_copy(q_parts[:, t, :, 2 * HD:3 * HD], q_parts[:, t, :, 0:HD]).then_inc(s["q_again"], 1)

            def split_fc():
                pool.wait_ge(s["raw_loaded"], 64)
                nc.gpsimd.tensor_copy(fc1_hi[:, :, :], fc1_raw.rearrange("p (k h) -> p k h", k=KD)).then_inc(s["split_step"], 1)
                nc.gpsimd.tensor_copy(fc2a_hi[:, :, :], fc2_raw[:, :, 0:P]).then_inc(s["split_step"], 1)
                for j in range(BT):
                    nc.gpsimd.tensor_copy(fc2b_hi[:, :, j, 0:SHARED - P], fc2_raw[:, :, P:SHARED]).then_inc(s["split_step"], 1)
                pool.wait_ge(s["split_step"], 2 + BT)
                nc.gpsimd.tensor_tensor(fc1_lo[:, :, :], fc1_raw.rearrange("p (k h) -> p k h", k=KD), fc1_hi[:, :, :].bitcast(F32), ALU.subtract).then_inc(s["fc_split"], 1)
                nc.gpsimd.tensor_tensor(fc2a_lo[:, :, :], fc2_raw[:, :, 0:P], fc2a_hi[:, :, :].bitcast(F32), ALU.subtract).then_inc(s["fc_split"], 1)
                for j in range(BT):
                    nc.gpsimd.tensor_tensor(fc2b_lo[:, :, j, 0:SHARED - P], fc2_raw[:, :, P:SHARED], fc2b_hi[:, :, j, 0:SHARED - P].bitcast(F32), ALU.subtract).then_inc(s["fc_split"], 1)

            rstd_of(0)
            high_again(0)
            split_fc()

            def move(b):
                pool.wait_ge(s["keys_low"], b + 1)
                pool.wait_ge(s["front_dve"], HEAD + 4 * b + 2)
                pool.wait_ge(s["score_mm"], HEAD + 6 * b)
                settle(pool, "pool_settled")
                nc.gpsimd.tensor_copy(keys[:, :], keys_new[:, :].bitcast(F32)).then_inc(s["keys_moved"], 1)
                pool.wait_ge(s["front_dve"], HEAD + 4 * (b + 1))
                pool.wait_ge(s["ring_mm"], HEAD + b * len(RING))
                settle(pool, "pool_settled")
                nc.gpsimd.tensor_copy(values[:, :, :], values_new[:, :, :]).then_inc(s["values_moved"], 1)

            def causal(b, f):
                pool.wait_ge(s["exp_done"], HEAD + 6 * b + f + 1)
                settle(pool, "pool_settled")
                if f in (2, 5):
                    v = p1[:, f // 3].rearrange("p a c t -> p (a c) t")
                else:
                    g = [0, 1, None, 2, 3][f]
                    v = p0[:, g].rearrange("p a c t -> p (a c) t")[:, :, 0:P]
                nc.gpsimd.affine_select(out=v, in_=v, compare_op=ALU.is_ge, fill=0.0, base=0,
                                        pattern=[[0, v.shape[1]], [1, P]], channel_multiplier=-1).then_inc(s["masked"], 1)

            def iteration(b, more):
                move(b)
                if more:
                    rstd_of(b + 1)
                for f in range(6):
                    causal(b, f)
                if more:
                    high_again(b + 1)

            with pool.Fori(0, B - 1) as b:
                iteration(b, True)
            iteration(B - 1, False)
            pool.wait_ge(s["fc_split"], 2 + BT)
            pool.wait_ge(s["masked"], 6 * B)
            pool.sem_inc(s["phase1_over"], 1)
            pool.wait_ge(s["phase1_over"], 4)

            with pool.Fori(0, TILES) as t:
                pool.wait_ge(s["expert_loaded"], 16 * BT * (t + 1))
                pool.wait_ge(s["unit_mm"], HEAD + (KH + KD) * t)
                settle(pool, "pool_settled")
                for j in range(BT):
                    nc.gpsimd.tensor_copy(fc2b_hi[:, :, j, SHARED - P:P], exp_raw[:, j]).then_inc(s["expert_hi"], 1)
                pool.wait_ge(s["expert_hi"], BT * (t + 1))
                for j in range(BT):
                    nc.gpsimd.tensor_tensor(fc2b_lo[:, :, j, SHARED - P:P], exp_raw[:, j], fc2b_hi[:, :, j, SHARED - P:P].bitcast(F32), ALU.subtract).then_inc(s["expert_split"], 1)
            pool.wait_ge(s["expert_split"], HEAD + BT * TILES)
            pool.sem_inc(s["phase2_over"], 1)

        @block.scalar
        def _(act):
            def relu(n):
                act.wait_ge(s["front_mm"], fill_at(n, FRONT, 0))
                nc.scalar.activation(h_t[0:A, :], front[0][0:A, 0:T], ACT.Relu, bias=vec[0:A, 4:5]).then_inc(s["front_act"], 1)

            def affine(n):
                act.wait_ge(s["front_mm"], fill_at(n, FRONT, 2))
                for k in range(KD):
                    last = nc.scalar.activation(norm_t[:, k, :], front[0][:, k * T:(k + 1) * T], ACT.Identity,
                                                bias=vec[:, 2 + k:3 + k], scale=vec[:, k:k + 1])
                last.then_inc(s["front_act"], 1)

            def q_copy(b, j):
                act.wait_ge(s["ring_mm"], HEAD + fill_at(b, RING, j))
                nc.scalar.activation(q_t[:, 4 * (j % 2):4 * (j % 2) + 4, (j // 2) * P:(j // 2 + 1) * P],
                                     ring[j % 2][:, :].rearrange("p (c t) -> p c t", c=4), ACT.Copy).then_inc(s["ring_act"], 1)

            def back(b, more):
                q_copy(b, 0)
                q_copy(b, 2)
                if more:
                    relu(b + 1)
                    affine(b + 1)
                act.wait_ge(s["ring_mm"], HEAD + fill_at(b, RING, 16))
                nc.scalar.activation(m_t[:, :], ring[0][:, 0:T], ACT.Copy).then_inc(s["ring_act"], 1)
                for f in range(6):
                    act.wait_ge(s["score_mm"], HEAD + 6 * b + f + 1)
                    src = score_bank[f % 2]
                    if f in (2, 5):
                        nc.scalar.activation(p1[:, f // 3].rearrange("p a c t -> p a (c t)"), src[:, :, :], ACT.Exp).then_inc(s["exp_done"], 1)
                    else:
                        g = [0, 1, None, 2, 3][f]
                        nc.scalar.activation(p0[:, g].rearrange("p a c t -> p a (c t)"), src[:, :, :], ACT.Exp).then_inc(s["exp_done"], 1)
                act.wait_ge(s["ring_mm"], HEAD + fill_at(b, RING, 19))
                nc.scalar.activation(att_t[:, :, :], ring[1][:, :].rearrange("p (k t) -> p k t", k=KD), ACT.Copy).then_inc(s["ring_act"], 1)

            act.wait_ge(s["front_loaded"], 80)
            relu(0)
            affine(0)
            act.wait_ge(s["sel_made"], 1)
            act.wait_ge(s["fc_split"], 2 + BT)
            with act.Fori(0, B - 1) as b:
                back(b, True)
            back(B - 1, False)
            act.wait_ge(s["ring_act"], HEAD + B * RING.count("act"))
            act.sem_inc(s["phase1_over"], 1)
            act.wait_ge(s["phase1_over"], 4)

            with act.Fori(0, TILES) as t:
                for m in range(KH):
                    act.wait_ge(s["unit_mm"], HEAD + (KH + KD) * t + m + 1)
                    if m >= 2:
                        act.wait_ge(s["act_ready"], HEAD + KH * t + m - 1)
                    else:
                        act.wait_ge(s["act_ready"], HEAD + KH * t)
                    nc.scalar.activation(g_raw[:, m % 2, :], bank[m % 4][:, :], ACT.Gelu, bias=fc1_bias[:, m:m + 1]).then_inc(s["raw_ready"], 1)
            act.wait_ge(s["raw_ready"], KH * TILES)
            act.sem_inc(s["phase2_over"], 1)
            act.wait_ge(s["phase2_over"], 4)

            with act.Fori(0, TILES) as t:
                for m in range(KH):
                    act.wait_ge(s["c_mm"], C_UNITS * t + 2 * m + 1)
                    if m >= 2:
                        act.wait_ge(s["prod_ready"], HEAD + KH * t + m - 1)
                    else:
                        act.wait_ge(s["prod_ready"], HEAD + KH * t)
                    nc.scalar.activation(sil[:, m % 2, :], bank[(2 * m) % 4][:, :], ACT.Silu, scale=SC_W1[:, m:m + 1]).then_inc(s["sil_ready"], 1)
                for layer in range(2):
                    for m in range(KH):
                        g = 2 * KH + layer * KH + m
                        act.wait_ge(s["c_mm"], C_UNITS * t + g + 1)
                        act.wait_ge(s["c_ready"], 3 * KH * t + (1 + layer) * KH + m - 1)
                        sc = (SC_H1, SC_H2)[layer]
                        nc.scalar.activation(h_raw[:, m % 2, :], bank[g % 4][:, :], ACT.Gelu, scale=sc[:, m:m + 1]).then_inc(s["c_act"], 1)

        @block.vector
        def _(dve):
            def layer_norm(n):
                dve.wait_ge(s["front_mm"], fill_at(n, FRONT, 1))
                nc.vector.tensor_tensor(u[:, :, :], front[1][:, :].rearrange("p (t d) -> p t d", t=NT), xtok[:, :, :], ALU.add).then_inc(s["front_dve"], 1)
                dve.wait_ge(s["front_dve"], HEAD + 4 * n + 1)
                for t in range(NT):
                    nc.vector.bn_stats(stats[:, t, :], u[:, t, :]).then_inc(s["stats_ready"], 1)
                dve.wait_ge(s["stats_ready"], NT * (n + 1))
                settle(dve, "dve_settled")
                for t in range(NT):
                    nc.vector.bn_aggr(moments[:, t, :], stats[:, t, :]).then_inc(s["moments_ready"], 1)
                dve.wait_ge(s["moments_ready"], NT * (n + 1))
                nc.vector.tensor_scalar(veps[:, :], moments[:, :, 1], EPS, None, ALU.add).then_inc(s["veps_ready"], 1)
                dve.wait_ge(s["rstd_ready"], n + 1)
                for t in range(NT):
                    nc.vector.tensor_scalar(norm[:, t, :], u[:, t, :], moments[:, t, 0:1], rstd[:, t:t + 1],
                                            ALU.subtract, ALU.mult).then_inc(s["norm_ready"], 1)

            def keys_of(n):
                dve.wait_ge(s["front_mm"], fill_at(n, FRONT, 3))
                dve.wait_ge(s["keys_moved"], HEAD + n)
                src = front[1]
                nc.vector.tensor_copy(keys_new[:, :], src[:, 0:T]).then_inc(s["keys_hi"], 1)
                dve.wait_ge(s["keys_hi"], n + 1)
                nc.vector.tensor_tensor(keys_new[32:64, :], src[32:64, 0:T], keys_new[32:64, :].bitcast(F32), ALU.subtract).then_inc(s["keys_low"], 1)
                nc.vector.tensor_tensor(keys_new[96:128, :], src[96:128, 0:T], keys_new[96:128, :].bitcast(F32), ALU.subtract).then_inc(s["front_dve"], 1)

            def queries_of(n, t):
                dve.wait_ge(s["front_mm"], fill_at(n, FRONT, 4 + t))
                dve.wait_ge(s["values_moved"], HEAD + n)
                src = front[t % 2]
                q = src[:, 0:D].rearrange("p (h c) -> p h c", h=NH)
                nc.vector.tensor_scalar(q_parts[:, t, :, 0:HD].bitcast(F32R), q, QSCALE, None, ALU.mult).then_inc(s["q_hi"], 1)
                dve.wait_ge(s["q_hi"], NT * n + t + 1)
                nc.vector.scalar_tensor_tensor(out=q_parts[:, t, :, HD:2 * HD].bitcast(F32R), in0=q, scalar=QSCALE, in1=q_parts[:, t, :, 0:HD],
                                               op0=ALU.mult, op1=ALU.subtract).then_inc(s["q_low"], 1)
                nc.vector.tensor_copy(values_new[:, t, 0:HD], src[:, D:D + HD]).then_inc(s["front_dve"], 1)

            def q_copy(b, j):
                dve.wait_ge(s["ring_mm"], HEAD + fill_at(b, RING, j))
                nc.vector.tensor_copy(q_t[:, 4 * (j % 2):4 * (j % 2) + 4, (j // 2) * P:(j // 2 + 1) * P],
                                      ring[j % 2][:, :].rearrange("p (c t) -> p c t", c=4)).then_inc(s["ring_dve"], 1)

            def max_of(b, j):
                dve.wait_ge(s["ring_mm"], HEAD + fill_at(b, RING, j))
                t, par, first, heads = max_fill(j)
                nc.vector.tensor_reduce(neg_max[:, t, first:first + heads, par], ring[j % 2][:, :].rearrange("p (h k) -> p h k", h=heads),
                                        AX.X, ALU.max, negate=True).then_inc(s["ring_dve"], 1)

            def back(b, more):
                q_copy(b, 1)
                q_copy(b, 3)
                for j in range(4, 10):
                    max_of(b, j)
                if more:
                    layer_norm(b + 1)
                for j in range(10, 16):
                    max_of(b, j)
                dve.wait_ge(s["ring_dve"], HEAD + b * RING.count("dve") + emptied(RING, 15)[1])
                nm = neg_max[:, :, :, :].rearrange("p t c a -> p t (c a)")
                for dup in range(2):
                    nc.vector.tensor_copy(m2[:, :, dup, 0:NH].bitcast(F32R), nm).then_inc(s["m2_hi"], 1)
                dve.wait_ge(s["m2_hi"], 2 * (b + 1))
                for dup in range(2):
                    nc.vector.tensor_tensor(m2[:, :, dup, NH:2 * NH].bitcast(F32R), nm, m2[:, :, dup, 0:NH], ALU.subtract).then_inc(s["m2_ready"], 1)
                if more:
                    keys_of(b + 1)
                for t in range(NT):
                    dve.wait_ge(s["ring_mm"], HEAD + fill_at(b, RING, 17 + t))
                    o = ring[(17 + t) % 2][:, 0:NH * (HD + 1)].rearrange("p (h c) -> p h c", h=NH)
                    nc.vector.reciprocal(recip[:, t, :], o[:, :, HD]).then_inc(s["recip_done"], 1)
                    dve.wait_ge(s["recip_done"], NT * b + t + 1)
                    nc.vector.tensor_tensor(att[:, t, :].rearrange("p (h c) -> p h c", h=NH), o[:, :, 0:HD],
                                            recip[:, t, :].rearrange("p (h c) -> p h c", c=1).broadcast_to([P, NH, HD]), ALU.mult).then_inc(s["ring_dve"], 1)
                if more:
                    queries_of(b + 1, 0)
                    queries_of(b + 1, 1)
                dve.wait_ge(s["resid_loaded"], 16 * (b + 1))
                dve.wait_ge(s["x1_stored"], HEAD + 16 * b)
                for m in range(KD):
                    dve.wait_ge(s["ring_mm"], HEAD + fill_at(b, RING, 20 + m))
                    nc.vector.scalar_tensor_tensor(out=x1[:, m, :], in0=ring[m % 2][:, 0:T], scalar=bf[:, m:m + 1], in1=resid[:, m, :],
                                                   op0=ALU.add, op1=ALU.add).then_inc(s["ring_dve"], 1)

            nc.vector.memset(h_t[A:A + 1, :], 1.0).then_inc(s["row_made"], 1)
            dve.wait_ge(s["front_loaded"], 80)
            dve.wait_ge(s["const_made"], 5)
            dve.wait_ge(s["const_loaded"], 96)
            layer_norm(0)
            keys_of(0)
            queries_of(0, 0)
            queries_of(0, 1)
            with dve.Fori(0, B - 1) as b:
                back(b, True)
            back(B - 1, False)
            dve.wait_ge(s["ring_dve"], HEAD + B * RING.count("dve"))
            dve.sem_inc(s["phase1_over"], 1)
            dve.wait_ge(s["phase1_over"], 4)

            nc.vector.memset(bits[:, :], 0.0).then_inc(s["bits_step"], 1)
            dve.wait_ge(s["ffn_loaded"], 16)
            with dve.Fori(0, TILES) as t:
                dve.wait_ge(s["xa_loaded"], 16 * (t + 1))
                dve.wait_ge(s["unit_mm"], HEAD + (KH + KD) * t)
                nc.vector.tensor_copy(xa_hi[:, :, :], xa[:, :, :]).then_inc(s["xa_hi"], 1)
                dve.wait_ge(s["xa_hi"], t + 1)
                nc.vector.tensor_tensor(xa_lo[:, :, :], xa[:, :, :], xa_hi[:, :, :].bitcast(F32), ALU.subtract).then_inc(s["xa_split"], 1)
                for m in range(KH):
                    dve.wait_ge(s["raw_ready"], KH * t + m + 1)
                    nc.vector.tensor_copy(g_hi[:, m, :], g_raw[:, m % 2, :]).then_inc(s["hi_ready"], 1)
                    dve.wait_ge(s["hi_ready"], KH * t + m + 1)
                    nc.vector.tensor_tensor(g_lo[:, m, :], g_raw[:, m % 2, :], g_hi[:, m, :].bitcast(F32), ALU.subtract).then_inc(s["act_ready"], 1)
                dve.wait_ge(s["bits_step"], t + 1)
                nc.vector.tensor_tensor(bits[:, :], bits[:, :], ffn_w[:, bass.ds(t * CHECK, CHECK)].bitcast(U32), ALU.bitwise_or).then_inc(s["bits_step"], 1)
                dve.wait_ge(s["bias_loaded"], 16 * (1 + BT) + 16 * BT * (t + 1))
                dve.wait_ge(s["y_stored"], HEAD + 16 * t)
                dve.wait_ge(s["unit_mm"], HEAD + (KH + KD) * t + KH + 1)
                nc.vector.tensor_scalar(y[:, 0, :], bank[0][:, :], fc2_bias[:, 0:1], None, ALU.add).then_inc(s["y_ready"], 1)
                dve.wait_ge(s["unit_mm"], HEAD + (KH + KD) * t + KH + 2)
                for j in range(BT):
                    nc.vector.tensor_scalar(y[:, 1, j * T:(j + 1) * T], bank[1][:, j * T:(j + 1) * T], fc2_bias[:, 1 + j:2 + j], None, ALU.add).then_inc(s["y_ready"], 1)
            dve.wait_ge(s["bits_step"], TILES + 1)
            nc.vector.tensor_scalar(bits_low[:, :], bits[:, :], 0xFFF, None, ALU.bitwise_and).then_inc(s["bits_step"], 1)
            dve.wait_ge(s["bits_step"], TILES + 2)
            nc.vector.tensor_reduce(bits_top[:, :], bits_low[:, :], AX.X, ALU.max).then_inc(s["bits_step"], 1)
            dve.wait_ge(s["bits_step"], TILES + 3)
            nc.vector.tensor_copy(low_bits[:, :], bits_top[:, :]).then_inc(s["bits_max"], 1)
            dve.wait_ge(s["bits_summed"], 1)
            nc.vector.tensor_copy(low_count[:, :], bank[2][0:1, 0:1]).then_inc(s["flag_ready"], 1)
            dve.wait_ge(s["y_ready"], HEAD + 3 * TILES)
            dve.wait_ge(s["flag_ready"], 1)
            dve.sem_inc(s["phase2_over"], 1)
            dve.wait_ge(s["phase2_over"], 4)

            def split(dst_hi, dst_lo, src, done):
                nc.vector.tensor_copy(dst_hi, src).then_inc(s["c_hi"], 1)
                dve.wait_ge(s["c_hi"], done + 1)
                nc.vector.tensor_tensor(dst_lo, src, dst_hi.bitcast(F32), ALU.subtract).then_inc(s["c_ready"], 1)

            with dve.Fori(0, TILES) as t:
                dve.wait_ge(s["yc_loaded"], 16 * (t + 1))
                nc.vector.tensor_copy(yc_hi[:, :, :], yc[:, :, :]).then_inc(s["yc_hi"], 1)
                dve.wait_ge(s["yc_hi"], t + 1)
                nc.vector.tensor_tensor(yc_lo[:, :, :], yc[:, :, :], yc_hi[:, :, :].bitcast(F32), ALU.subtract).then_inc(s["yc_split"], 1)
                for m in range(KH):
                    dve.wait_ge(s["sil_ready"], KH * t + m + 1)
                    dve.wait_ge(s["c_mm"], C_UNITS * t + 2 * m + 2)
                    dve.wait_ge(s["c_act"], HEAD + 2 * KH * t)
                    nc.vector.scalar_tensor_tensor(out=h_raw[:, m % 2, :], in0=bank[(2 * m + 1) % 4][:, :], scalar=SC_W2[:, m:m + 1],
                                                   in1=sil[:, m % 2, :], op0=ALU.mult, op1=ALU.mult).then_inc(s["prod_ready"], 1)
                    dve.wait_ge(s["prod_ready"], HEAD + KH * t + m + 1)
                    split(h_hi[0][:, m, :], h_lo[0][:, m, :], h_raw[:, m % 2, :], 3 * KH * t + m)
                for layer in range(2):
                    for m in range(KH):
                        dve.wait_ge(s["c_act"], HEAD + 2 * KH * t + layer * KH + m + 1)
                        split(h_hi[1 - layer][:, m, :], h_lo[1 - layer][:, m, :], h_raw[:, m % 2, :], 3 * KH * t + (1 + layer) * KH + m)
                dve.wait_ge(s["resid2_loaded"], 16 * (t + 1))
                dve.wait_ge(s["out_stored"], HEAD + 16 * t)
                for m in range(KD):
                    g = 4 * KH + m
                    dve.wait_ge(s["c_mm"], C_UNITS * t + g + 1)
                    nc.vector.scalar_tensor_tensor(out=outs[:, m, :], in0=bank[g % 4][:, :], scalar=SC_W3[:, m:m + 1], in1=resid2[:, m, :],
                                                   op0=ALU.mult, op1=ALU.add).then_inc(s["out_ready"], 1)

        @block.tensor
        def _(pe):
            mm = nc.tensor.matmul

            def front_free(n, j):
                if j >= 2:
                    wait_emptied(pe, FRONT, s["front_act"], s["front_dve"], n, j - 2)
                elif not (isinstance(n, int) and n == 0):
                    wait_emptied(pe, FRONT, s["front_act"], s["front_dve"], n - 1, len(FRONT) + j - 2)

            def ring_free(b, j):
                if j >= 2:
                    wait_emptied(pe, RING, s["ring_act"], s["ring_dve"], b, j - 2)
                else:
                    pe.wait_ge(s["ring_dve"], HEAD + b * RING.count("dve"))

            def adapter_in(n):
                pe.wait_ge(s["front_loaded"], 80 * (n + 1))
                front_free(n, 0)
                for k in range(KD):
                    last = mm(front[0][0:A, 0:T], w1c[:, k, :], xt[:, k, :], start=k == 0, stop=k == KD - 1)
                last.then_inc(s["front_mm"], 1)

            def adapter_out(n):
                pe.wait_ge(s["front_act"], HEAD + 2 * n + 1)
                front_free(n, 1)
                for t in range(NT):
                    last = mm(front[1][:, t * D:(t + 1) * D], h_t[:, t * P:(t + 1) * P], w2c[:, :], start=True, stop=True)
                last.then_inc(s["front_mm"], 1)

            def norm_transposed(n):
                pe.wait_ge(s["norm_ready"], NT * (n + 1))
                front_free(n, 2)
                for k in range(KD):
                    for t in range(NT):
                        last = nc.tensor.transpose(front[0][:, k * T + t * P:k * T + (t + 1) * P], norm[:, t, k * P:(k + 1) * P], ident[:, :])
                last.then_inc(s["front_mm"], 1)

            def keys_mm(n):
                pe.wait_ge(s["front_act"], HEAD + 2 * (n + 1))
                front_free(n, 3)
                for k in range(KD):
                    last = mm(front[1][:, 0:T], wk[:, k, :], norm_t[:, k, :], start=k == 0, stop=k == KD - 1)
                last.then_inc(s["front_mm"], 1)

            def queries_mm(n, t):
                front_free(n, 4 + t)
                for k in range(KD):
                    last = mm(front[t % 2][:, 0:D + HD], norm_t[:, k, t * P:(t + 1) * P], wqv[:, k, :], start=k == 0, stop=k == KD - 1)
                last.then_inc(s["front_mm"], 1)

            def q_transposed(b, j):
                t = j // 2
                pe.wait_ge(s["q_low"], NT * b + t + 1)
                pe.wait_ge(s["q_again"], NT * b + t + 1)
                ring_free(b, j)
                for c in range(4):
                    pair = 4 * (j % 2) + c
                    last = nc.tensor.transpose(ring[j % 2][:, c * P:(c + 1) * P], q_parts[:, t, 2 * pair:2 * pair + 2, :], ident[:, :])
                last.then_inc(s["ring_mm"], 1)

            def half_rows(par):
                return slice(SLOT * par, SLOT * (par + 1))

            def max_scores(b, j):
                t, par, first, heads = max_fill(j)
                if j == 4:
                    pe.wait_ge(s["ring_act"], HEAD + b * RING.count("act") + 2)
                    pe.wait_ge(s["ring_dve"], HEAD + b * RING.count("dve") + 2)
                    pe.wait_ge(s["keys_moved"], HEAD + b + 1)
                ring_free(b, j)
                r = half_rows(par)
                n = P * (t + 1)
                for c in range(heads):
                    mm(ring[j % 2][:, c * n:(c + 1) * n], q_t[r, first + c, t * P:(t + 1) * P], keys[r, 0:n], start=c == 0, stop=False)
                diag = ring[j % 2][:, :].rearrange("p (h k) -> p h k", h=heads)[:, :, n - P:n]
                mm(diag, ident_b[:, :], mask[:, 0:heads, :], start=False, stop=True).then_inc(s["ring_mm"], 1)

            def max_transposed(b):
                pe.wait_ge(s["m2_ready"], 2 * (b + 1))
                ring_free(b, 16)
                for t in range(NT):
                    last = nc.tensor.transpose(ring[0][:, t * P:(t + 1) * P], m2[:, t, :, :].rearrange("p a c -> p (a c)"), ident[:, :])
                last.then_inc(s["ring_mm"], 1)

            def scores(b, f):
                if f == 0:
                    pe.wait_ge(s["ring_act"], HEAD + b * RING.count("act") + 3)
                if f >= 2:
                    pe.wait_ge(s["exp_done"], HEAD + 6 * b + f - 1)
                else:
                    pe.wait_ge(s["exp_done"], HEAD + 6 * b)
                dst = score_bank[f % 2]
                for par in range(2):
                    r = half_rows(par)
                    if f in (2, 5):
                        first, pairs, k0, q0 = 4 * (f // 3), 4, P, P
                    else:
                        first, pairs, k0, q0 = 2 * [0, 1, None, 2, 3][f], 2, 0, 0
                    n = T - q0
                    mm(dst[:, par, :].rearrange("p (c t) -> p c t", c=pairs), keys[r, k0:k0 + P], q_t[r, first:first + pairs, q0:T], start=True, stop=False)
                    for c in range(pairs):
                        last = mm(dst[:, par, c * n:(c + 1) * n], sel[r, 2 * (first + c) + par, :], m_t[r, q0:T], start=False, stop=c == pairs - 1)
                last.then_inc(s["score_mm"], 1)

            def products(b, half_):
                pe.wait_ge(s["masked"], 6 * b + (3, 6)[half_])
                if half_ == 0:
                    pe.wait_ge(s["values_moved"], HEAD + b + 1)
                    ring_free(b, 17)
                    ring_free(b, 18)
                for h in range(8 * half_, 8 * half_ + 8):
                    pair, par = h // 2, h % 2
                    c = slice(h * (HD + 1), (h + 1) * (HD + 1))
                    early = p0[:, pair // 2, par, pair % 2, :]
                    mm(ring[1][:, c], early[:, 0:P], values[:, 0, :], start=True, stop=True)
                    mm(ring[0][:, c], early[:, P:T], values[:, 0, :], start=True, stop=False)
                    last = mm(ring[0][:, c], p1[:, pair // 4, par, pair % 4, :], values[:, 1, :], start=False, stop=True)
                if half_ == 1:
                    last.then_inc(s["ring_mm"], 2)

            def att_transposed(b):
                pe.wait_ge(s["ring_dve"], HEAD + b * RING.count("dve") + emptied(RING, 18)[1])
                for k in range(KD):
                    for t in range(NT):
                        last = nc.tensor.transpose(ring[1][:, k * T + t * P:k * T + (t + 1) * P], att[:, t, k * P:(k + 1) * P], ident[:, :])
                last.then_inc(s["ring_mm"], 1)

            def project(b):
                pe.wait_ge(s["ring_act"], HEAD + (b + 1) * RING.count("act"))
                for m in range(KD):
                    for k in range(KD):
                        last = mm(ring[m % 2][:, 0:T], wf[:, k, m * P:(m + 1) * P], att_t[:, k, :], start=k == 0, stop=k == KD - 1)
                    last.then_inc(s["ring_mm"], 1)

            def back(b, more):
                for j in range(4):
                    q_transposed(b, j)
                if more:
                    adapter_in(b + 1)
                for j in range(4, 10):
                    max_scores(b, j)
                if more:
                    adapter_out(b + 1)
                for j in range(10, 16):
                    max_scores(b, j)
                if more:
                    norm_transposed(b + 1)
                max_transposed(b)
                if more:
                    keys_mm(b + 1)
                for f in range(4):
                    scores(b, f)
                products(b, 0)
                for f in range(4, 6):
                    scores(b, f)
                products(b, 1)
                if more:
                    queries_mm(b + 1, 0)
                att_transposed(b)
                if more:
                    queries_mm(b + 1, 1)
                project(b)

            pe.wait_ge(s["const_loaded"], 96)
            pe.wait_ge(s["const_made"], 5)
            pe.wait_ge(s["sel_made"], 2)
            pe.wait_ge(s["row_made"], 1)
            adapter_in(0)
            adapter_out(0)
            norm_transposed(0)
            keys_mm(0)
            queries_mm(0, 0)
            queries_mm(0, 1)
            with pe.Fori(0, B - 1) as b:
                back(b, True)
            back(B - 1, False)
            pe.wait_ge(s["ring_mm"], HEAD + B * len(RING))
            pe.sem_inc(s["phase1_over"], 1)
            pe.wait_ge(s["phase1_over"], 4)

            with pe.Fori(0, TILES) as t:
                base = (KH + KD) * t
                pe.wait_ge(s["xa_split"], HEAD + t + 1)
                for m in range(KH):
                    if m >= 4:
                        pe.wait_ge(s["raw_ready"], KH * t + m - 3)
                    elif m < 2:
                        pe.wait_ge(s["y_ready"], HEAD + 3 * t)
                    cols = slice(m * P, (m + 1) * P)
                    passes = [(w, v, k) for w, v in ((fc1_hi, xa_hi), (fc1_hi, xa_lo), (fc1_lo, xa_hi)) for k in range(KD)]
                    for i, (w, v, k) in enumerate(passes):
                        last = mm(bank[m % 4][:, :], w[:, k, cols], v[:, k, :], start=i == 0, stop=i == len(passes) - 1)
                    last.then_inc(s["unit_mm"], 1)
                for k in range(KH):
                    pe.wait_ge(s["act_ready"], HEAD + KH * t + k + 1)
                    if k == 0:
                        pe.wait_ge(s["raw_ready"], KH * t + 6)
                    for i, (w, v) in enumerate(((fc2a_hi, g_hi), (fc2a_hi, g_lo), (fc2a_lo, g_hi))):
                        last = mm(bank[0][:, :], w[:, k, :], v[:, k, :], start=k == 0 and i == 0, stop=k == KH - 1 and i == 2)
                last.then_inc(s["unit_mm"], 1)
                pe.wait_ge(s["expert_split"], HEAD + BT * (t + 1))
                for j in range(BT):
                    for k in range(KH):
                        for i, (w, v) in enumerate(((fc2b_hi, g_hi), (fc2b_hi, g_lo), (fc2b_lo, g_hi))):
                            last = mm(bank[1][:, j * T:(j + 1) * T], w[:, k, j, :], v[:, k, j * T:(j + 1) * T],
                                      start=k == 0 and i == 0, stop=k == KH - 1 and i == 2)
                last.then_inc(s["unit_mm"], 1)
            pe.wait_ge(s["bits_max"], 1)
            mm(bank[2][0:1, 0:1], low_bits[:, :], ones[:, :], start=True, stop=True).then_inc(s["bits_summed"], 1)
            pe.wait_ge(s["flag_ready"], 1)
            pe.sem_inc(s["phase2_over"], 1)
            pe.wait_ge(s["phase2_over"], 4)

            def ffn(dt):
                def w_at(at, k, width, m):
                    w = ffn_w[:, at + k * width + m * P:at + k * width + (m + 1) * P]
                    return w if dt is F32R else w.bitcast(dt)

                def v_at(v, k):
                    return v[:, k, :] if dt is F32R else v[:, k, :].bitcast(dt)

                def unit(t, g, at, width, m, hi, lo, tiles, ready):
                    for k in range(tiles):
                        if ready is not None and m == 0:
                            pe.wait_ge(s["c_ready"], ready + k + 1)
                        for i, v in enumerate((hi, lo)):
                            last = mm(bank[g % 4][:, :], w_at(at, k, width, m), v_at(v, k), start=k == 0 and i == 0, stop=k == tiles - 1 and i == 1)
                    last.then_inc(s["c_mm"], 1)

                with pe.Fori(0, TILES) as t:
                    pe.wait_ge(s["yc_split"], HEAD + t + 1)
                    pe.wait_ge(s["out_ready"], HEAD + KD * t)
                    for m in range(KH):
                        if m >= 2:
                            pe.wait_ge(s["sil_ready"], KH * t + m - 1)
                        unit(t, 2 * m, W1_AT, HID, m, yc_hi, yc_lo, KD, None)
                        if m >= 2:
                            pe.wait_ge(s["prod_ready"], HEAD + KH * t + m - 1)
                        unit(t, 2 * m + 1, W2_AT, HID, m, yc_hi, yc_lo, KD, None)
                    for layer, at in enumerate((H1_AT, H2_AT)):
                        for m in range(KH):
                            if layer == 0 and m < 4:
                                pe.wait_ge(s["prod_ready"], HEAD + KH * t + (7, 7, 8, 8)[m])
                            else:
                                pe.wait_ge(s["c_act"], HEAD + 2 * KH * t + layer * KH + m - 3)
                            unit(t, 2 * KH + layer * KH + m, at, HID, m, h_hi[layer], h_lo[layer], KH, 3 * KH * t + layer * KH)
                    for m in range(KD):
                        pe.wait_ge(s["c_act"], HEAD + 2 * KH * t + 2 * KH + m - 3)
                        unit(t, 4 * KH + m, W3_AT, D, m, h_hi[0], h_lo[0], KH, 3 * KH * t + 2 * KH)

            with pe.register("low_bits_found") as found:
                nc.tensor.reg_load(found, low_count[0:1, 0:1])
                with pe.If_ne(found, 0):
                    ffn(F32)
                with pe.Else():
                    ffn(F32R)


def tiles(a):
    a = np.ascontiguousarray(a)
    return np.ascontiguousarray(a.reshape(-1, P, a.shape[-1]).transpose(1, 0, 2))


def kernel(**inputs):
    import ml_dtypes
    import concourse.bacc as _bacc
    from concourse.bass_utils import run_bass_kernel_spmd as _run

    g = {k: np.asarray(v) for k, v in inputs.items()}
    z = np.zeros
    x = g["x"]
    a = {}
    a["x_t"] = tiles(x.reshape(TOK, D).T)
    a["x_tok"] = x.reshape(B, NT, P, D).transpose(0, 2, 1, 3)
    a["lang"] = g["itok_B_0_8"].reshape(1, B)
    a["expert"] = g["itok_B_0_15"].reshape(1, B)
    a["cond_w1"] = g["L0_cond_W1"].reshape(L, KD, P, A).transpose(0, 2, 1, 3)
    a["cond_w2"] = np.concatenate([g["L0_cond_W2"], g["L0_cond_b2"][:, None, :]], 1)
    vec = z((L, P, 5), np.float32)
    vec[:, :, 0:2] = g["L0_cond_gamma"].reshape(L, KD, P).transpose(0, 2, 1)
    vec[:, :, 2:4] = g["L0_cond_beta"].reshape(L, KD, P).transpose(0, 2, 1)
    vec[:, 0:A, 4] = g["L0_cond_b1"]
    a["cond_vec"] = vec
    a["w_qv"] = tiles(np.concatenate([g["L0_attn_Wq"].T, g["L0_attn_Wv"].T], 1))
    wk = z((D, P), np.float32)
    for at in (0, 16, 32, 64, 80, 96):
        wk[:, at:at + HD] = g["L0_attn_Wk"].T
    a["w_k"] = tiles(wk)
    a["w_f"] = tiles(g["L0_attn_Wf"].T)
    a["b_f"] = g["L0_attn_bf"].reshape(KD, P).T
    a["ident_d"] = np.eye(P, dtype=np.float32)
    q, k = np.arange(P)[:, None, None], np.arange(P)[None, None, :]
    a["mask_d"] = np.broadcast_to(np.where(k > q, -1e30, 0.0), (P, 4, P)).astype(ml_dtypes.bfloat16)
    sel = z((P, NH, P), np.float32)
    for h in range(NH):
        sel[[h, h + NH, h + SLOT, h + SLOT + NH], h, :] = 1.0
    a["sel_d"] = sel.reshape(P, NH * P)
    a["fc1_w"] = tiles(g["L0_cond2_fc1_w"].T).reshape(P, KD * HID)
    a["fc1_b"] = g["L0_cond2_fc1_b"].reshape(KH, P).T
    a["fc2_w"] = tiles(g["L0_cond2_fc2_w"].T)
    fc2_b = z((2, P, 1), np.float32)
    fc2_b.reshape(-1)[0:SHARED] = g["L0_cond2_fc2_b"]
    a["fc2_b"] = fc2_b
    a["exp_w"] = g["L0_cond2_experts_w"].reshape(E, PART, KH, P).transpose(0, 3, 2, 1)
    a["exp_b"] = g["L0_cond2_experts_b"].reshape(E, PART, 1)
    a["ffn_d"] = np.concatenate([tiles(g[f"L0_ffn_{n}_w"].T).reshape(P, -1) for n in ("w1", "w2", "h1", "h2", "w3")], 1)
    a["ffn_s"] = np.concatenate([g[f"L0_ffn_{n}_s"].reshape(-1, P).T for n in ("w1", "w2", "h1", "h2", "w3")], 1)

    nc = _bacc.Bacc("TRN2", target_bir_lowering=False, num_devices=1)
    arrays, args = {}, {}
    for name, v in a.items():
        v = np.ascontiguousarray(v)
        arrays[f"in_{name}"] = v
        args[name] = nc.dram_tensor(f"in_{name}", v.shape, mybir.dt.from_np(v.dtype), kind="ExternalInput").ap()
    out_t = nc.dram_tensor("out_t", (P, KD, TOK), F32, kind="ExternalOutput").ap()
    build(nc, out_t=out_t, **args)
    r = _run(nc, [arrays], core_ids=[0])
    got = r.results[0]["out_t"]
    return np.ascontiguousarray(got.transpose(1, 0, 2).reshape(D, TOK).T.reshape(B, T, D))
```

```python
from contextlib import ExitStack

import numpy as np

import concourse.bass as bass
from concourse import mybir

F32 = mybir.dt.float32
F32R = mybir.dt.float32r
BF16 = mybir.dt.bfloat16
I32 = mybir.dt.int32
U32 = mybir.dt.uint32
ALU = mybir.AluOpType
ACT = mybir.ActivationFunctionType
AX = mybir.AxisListType

P = 128
B, T, D = 16, 256, 256
KD = D // P
NT = T // P
TOK = B * T
L, A = 10, 64
NH, HD = 16, 16
NP = NH // 2
SLOT = 64
HID = 1024
KH = HID // P
E, PART = 16, 64
SHARED = D - PART
EPS = 1e-5
QSCALE = HD ** -0.5
HEAD = 1
HEAD_STARTED = "xa_split expert_split y_ready yc_split out_ready unit_mm prod_ready act_ready y_stored c_act out_stored".split()

TW = 512
TILES = TOK // TW
BT = TW // T

W1_AT = 0
W2_AT = W1_AT + KD * HID
H1_AT = W2_AT + KD * HID
H2_AT = H1_AT + KH * HID
W3_AT = H2_AT + KH * HID
FFN_COLS = W3_AT + KH * D
LATE = (2, 5)
C_UNITS = 4 * KH + KD
FILLS = 6
CHECK = FFN_COLS // TILES

def max_fill(f):
    return (0, 4 * f, 4) if f < 2 else (1, 2 * (f - 2), 2)


def score_fill(f):
    if f in LATE:
        return 4 * LATE.index(f), 4, P, P
    return 2 * [0, 1, None, 2, 3][f], 2, 0, 0


def build(nc, x_t, x_tok, lang, expert, cond_w1, cond_w2, cond_vec, w_qv, w_k, w_f, b_f, ident_d, mask_d, sel_d,
          fc1_w, fc1_b, fc2_w, fc2_b, exp_w, exp_b, ffn_d, ffn_s, out_t):
    ctx = ExitStack()
    with ctx:
        def sb(name, shape, dt=F32, where=ctx):
            return where.enter_context(nc.sbuf_tensor(name, shape, dt))

        def sem(name):
            return ctx.enter_context(nc.semaphore(name))

        bank = [ctx.enter_context(nc.psum_tensor(f"bank{i}", [P, 512], F32)) for i in range(4)]
        pair_bank = [ctx.enter_context(nc.psum_tensor(f"pair{i}", [P, 2, 512], F32)) for i in range(2)]
        ring = bank[0:2]
        side = bank[2:4]
        banks = [b[:, :] for b in bank] + [b[:, i, :] for b in pair_bank for i in range(2)]

        ffn_scratch = nc.dram_tensor("ffn_scratch", (P, FFN_COLS), F32).ap()
        x1_scratch = nc.dram_tensor("x1_scratch", (P, KD, TOK), F32).ap()
        y_scratch = nc.dram_tensor("y_scratch", (P, KD, TOK), F32).ap()

        ffn_w = sb("ffn_w", [P, FFN_COLS], F32R)
        fc1_bias = sb("fc1_bias", [P, KH])
        fc2_bias = sb("fc2_bias", [P, 1 + BT])
        scales = sb("scales", [P, 4 * KH + KD])
        low_bits = sb("low_bits", [P, 1])
        low_count = sb("low_count", [1, 1], I32)
        ones = sb("ones", [P, 1])
        SC_W1, SC_W2, SC_H1, SC_H2 = (scales[:, i * KH:(i + 1) * KH] for i in range(4))

        SC_W3 = scales[:, 4 * KH:4 * KH + KD]

        s = {}
        for name in """
                sp_settled pool_settled dve_settled raw_loaded const_loaded sel_loaded ffn_copied ffn_loaded fc_split split_step const_made sel_made row_made
                front_loaded hidden_mm hidden_out adapted_mm u_out norm_t_mm norm_t_out keys_mm keys_out qv_mm qv_out
                stats_ready moments_ready veps_ready rstd_ready norm_ready
                keys_hi keys_low q_hi q_low q_again keys_moved values_moved
                q_t_mm q_t_act q_t_dve max_mm max_out m2_hi m2_ready max_t_mm max_t_out
                score_mm exp_done masked early_mm early_out late_mm late_out
                pv_t_mm recip_done att_out att_t_mm att_t_out proj_mm x1_out resid_loaded x1_stored
                phase1_over phase2_over
                xa_loaded xa_hi xa_split expert_loaded expert_hi expert_split bias_loaded
                unit_mm unit_act unit_dve raw_ready hi_ready act_ready y_hi y_ready y_stored
                bits_step bits_max bits_summed flag_ready
                yc_loaded yc_hi yc_split resid2_loaded sil_ready prod_ready c_mm c_act c_dve c_raw c_hi c_ready
                out_ready out_stored""".split():
            s[name] = sem(name)

        early = ExitStack()
        fc1_hi = sb("fc1_hi", [P, KD, HID], F32R, early)
        fc1_lo = sb("fc1_lo", [P, KD, HID], F32R, early)
        fc2a_hi = sb("fc2a_hi", [P, KH, P], F32R, early)
        fc2a_lo = sb("fc2a_lo", [P, KH, P], F32R, early)
        fc2b_hi = sb("fc2b_hi", [P, KH, BT, P], F32R, early)
        fc2b_lo = sb("fc2b_lo", [P, KH, BT, P], F32R, early)

        one = ExitStack()
        xt = sb("xt", [P, KD, T], F32, one)
        xtok = sb("xtok", [P, NT, D], F32, one)
        w1c = sb("w1c", [P, KD, A], F32, one)
        w2c = sb("w2c", [A + 1, D], F32, one)
        vec = sb("vec", [P, 5], F32, one)
        wqv = sb("wqv", [P, KD, D + HD], F32, one)
        wk = sb("wk", [P, KD, P], F32, one)
        wf = sb("wf", [P, KD, D], F32, one)
        bf = sb("bf", [P, KD], F32, one)
        ident = sb("ident", [P, P], F32, one)
        ident_b = sb("ident_b", [P, P], BF16, one)
        mask = sb("mask", [P, 4, P], BF16, one)
        sel = sb("sel", [P, NH], F32R, one)
        sel_raw = sb("sel_raw", [P, NH], F32, one)
        h_t = sb("h_t", [A + 1, T], F32, one)
        u = sb("u", [P, NT, D], F32, one)
        stats = sb("stats", [P, NT, 6], F32, one)
        moments = sb("moments", [P, NT, 2], F32, one)
        veps = sb("veps", [P, NT], F32, one)
        half = sb("half", [P, NT], F32, one)
        rstd = sb("rstd", [P, NT], F32, one)
        norm = sb("norm", [P, NT, D], F32, one)
        norm_t = sb("norm_t", [P, KD, T], F32, one)
        q_parts = sb("q_parts", [P, NT, NH, SLOT], F32, one)
        q_t = sb("q_t", [P, NP, T], F32R, one)
        keys_new = sb("keys_new", [P, T], F32R, one)
        keys = sb("keys", [P, T], F32R, one)
        values_new = sb("values_new", [P, NT, 32], F32, one)
        values = sb("values", [P, NT, 32], F32, one)
        pv = sb("pv", [P, 4, T], F32, one)
        neg_max = sb("neg_max", [P, NT, NP, 2], F32, one)
        m2 = sb("m2", [P, NT, 2, SLOT], F32, one)
        m_t = sb("m_t", [P, T], F32R, one)
        p0 = sb("p0", [P, 4, 2, 2, T], F32, one)
        p1 = sb("p1", [P, 2, 2, 4, P], F32, one)
        p0_flat = p0[:, :, :, :, :].rearrange("p a b c t -> p (a b c t)")
        fc1_raw = p0_flat[:, 0:KD * HID]
        fc2_raw = p0_flat[:, KD * HID:KD * HID + KH * SHARED].rearrange("p (k o) -> p k o", k=KH)
        recip = sb("recip", [P, NT, NH], F32, one)
        att = sb("att", [P, NT, D], F32, one)
        att_t = sb("att_t", [P, KD, T], F32, one)
        resid = sb("resid", [P, KD, T], F32, one)
        x1 = sb("x1", [P, KD, T], F32, one)
        one.close()

        two = ExitStack()
        xa = sb("xa", [P, KD, TW], F32, two)
        xa_hi = sb("xa_hi_b", [P, KD, TW], F32R, two)
        xa_lo = sb("xa_lo_b", [P, KD, TW], F32R, two)
        exp_raw = sb("exp_raw", [P, BT, KH, PART], F32, two)
        g_hi = sb("g_hi", [P, KH, TW], F32R, two)
        g_lo = sb("g_lo", [P, KH, TW], F32R, two)
        g_raw = sb("g_raw", [P, 2, TW], F32, two)
        y = sb("y", [P, KD, TW], F32, two)
        bits = sb("bits", [P, CHECK], U32, two)
        bits_low = sb("bits_low", [P, CHECK], U32, two)
        bits_top = sb("bits_top", [P, 1], U32, two)
        two.close()
        early.close()

        three = ExitStack()
        yc = sb("yc", [P, KD, TW], F32, three)
        yc_hi = sb("yc_hi_b", [P, KD, TW], F32R, three)
        yc_lo = sb("yc_lo_b", [P, KD, TW], F32R, three)
        h_hi = [sb(f"h{i}_hi", [P, KH, TW], F32R, three) for i in range(2)]
        h_lo = [sb(f"h{i}_lo", [P, KH, TW], F32R, three) for i in range(2)]
        sil = sb("sil", [P, 2, TW], F32, three)
        h_raw = sb("h_raw", [P, 2, TW], F32, three)
        resid2 = sb("resid2", [P, KD, TW], F32, three)
        outs = sb("outs", [P, KD, TW], F32, three)
        three.close()

        block = ctx.enter_context(nc.Block())

        def is_first(n):
            return isinstance(n, int) and n == 0

        def is_last(n):
            return isinstance(n, int) and n == B - 1

        def settle(eng, name):
            eng.sem_inc(s[name], 1)

        @block.sync
        def _(sp):
            def load_front(n):
                l = sp.value_load(lang[0:1, bass.ds(n, 1)], min_val=0, max_val=L - 1)
                if not is_first(n):
                    sp.wait_ge(s["adapted_mm"], n)
                sp.dma_start(xt[:, :, :], x_t[:, :, bass.ds(n * T, T)]).then_inc(s["front_loaded"], 16)
                sp.dma_start(w1c[:, :, :], cond_w1[bass.ds(l, 1)].rearrange("a p k h -> p (a k) h")).then_inc(s["front_loaded"], 16)
                sp.dma_start(w2c[:, :], cond_w2[bass.ds(l, 1)].rearrange("a p h -> p (a h)")).then_inc(s["front_loaded"], 16)
                if not is_first(n):
                    sp.wait_ge(s["u_out"], n)
                    sp.wait_ge(s["norm_t_out"], n)
                    settle(sp, "sp_settled")
                sp.dma_start(xtok[:, :, :], x_tok[bass.ds(n, 1)].rearrange("a p t d -> p (a t) d")).then_inc(s["front_loaded"], 16)
                sp.dma_start(vec[:, :], cond_vec[bass.ds(l, 1)].rearrange("a p c -> p (a c)")).then_inc(s["front_loaded"], 16)

            def load_resid(b):
                if not is_first(b):
                    sp.wait_ge(s["x1_out"], KD * b)
                sp.dma_start(resid[:, :, :], x_t[:, :, bass.ds(b * T, T)]).then_inc(s["resid_loaded"], 16)

            def store_x1(b):
                sp.wait_ge(s["x1_out"], KD * (b + 1))
                sp.dma_start(x1_scratch[:, :, bass.ds(b * T, T)], x1[:, :, :]).then_inc(s["x1_stored"], 16)

            load_front(0)
            sp.dma_start(ident[:, :], ident_d).then_inc(s["const_loaded"], 16)
            sp.dma_start(wqv[:, :, :], w_qv).then_inc(s["const_loaded"], 16)
            sp.dma_start(wk[:, :, :], w_k).then_inc(s["const_loaded"], 16)
            sp.dma_start(wf[:, :, :], w_f).then_inc(s["const_loaded"], 16)
            sp.dma_start(bf[:, :], b_f).then_inc(s["const_loaded"], 16)
            sp.dma_start(mask[:, :, :], mask_d).then_inc(s["const_loaded"], 16)
            sp.dma_start(sel_raw[:, :], sel_d).then_inc(s["sel_loaded"], 16)
            load_resid(0)
            sp.dma_start(fc1_raw, fc1_w).then_inc(s["raw_loaded"], 16)
            sp.dma_start(fc2_raw, fc2_w).then_inc(s["raw_loaded"], 16)
            sp.dma_start(fc1_bias[:, :], fc1_b).then_inc(s["raw_loaded"], 16)
            sp.dma_start(scales[:, :], ffn_s).then_inc(s["raw_loaded"], 16)
            load_front(1)
            sp.dma_start(ffn_scratch, ffn_d).then_inc(s["ffn_copied"], 16)
            sp.wait_ge(s["ffn_copied"], 16)
            sp.dma_start(ffn_w[:, :].bitcast(F32), ffn_scratch).then_inc(s["ffn_loaded"], 16)
            with sp.Fori(0, B - 2) as b:
                load_front(b + 2)
                store_x1(b)
                load_resid(b + 1)
            store_x1(B - 2)
            load_resid(B - 1)
            store_x1(B - 1)
            sp.wait_ge(s["x1_stored"], 16 * B)
            sp.wait_ge(s["phase1_over"], 4)

            def load_expert(t):
                for j in range(BT):
                    e = sp.value_load(expert[0:1, bass.ds(t * BT + j, 1)], min_val=0, max_val=E - 1)
                    sp.dma_start(exp_raw[:, j], exp_w[bass.ds(e, 1)].rearrange("a p k h -> p (a k) h")).then_inc(s["expert_loaded"], 16)
                    sp.dma_start(fc2_bias[SHARED - P:P, 1 + j:2 + j], exp_b[bass.ds(e, 1)].rearrange("a p o -> p (a o)")).then_inc(s["bias_loaded"], 16)

            sp.dma_start(fc2_bias[:, 0:1], fc2_b[0]).then_inc(s["bias_loaded"], 16)
            for j in range(BT):
                sp.dma_start(fc2_bias[0:SHARED - P, 1 + j:2 + j], fc2_b[1, 0:SHARED - P]).then_inc(s["bias_loaded"], 16)

            def load_x(t):
                if not is_first(t):
                    sp.wait_ge(s["xa_split"], HEAD + t)
                sp.dma_start(xa[:, :, :], x1_scratch[:, :, bass.ds(t * TW, TW)]).then_inc(s["xa_loaded"], 16)

            def cond2_tile(t, more):
                if not is_first(t):
                    sp.wait_ge(s["expert_split"], HEAD + BT * t)
                    sp.wait_ge(s["y_ready"], HEAD + (1 + BT) * t)
                    settle(sp, "sp_settled")
                load_expert(t)
                if more:
                    load_x(t + 1)
                sp.wait_ge(s["y_ready"], HEAD + (1 + BT) * (t + 1))
                sp.dma_start(y_scratch[:, :, bass.ds(t * TW, TW)], y[:, :, :]).then_inc(s["y_stored"], 16)

            load_x(0)
            with sp.Fori(0, TILES - 1) as t:
                cond2_tile(t, True)
            cond2_tile(TILES - 1, False)
            sp.wait_ge(s["y_stored"], HEAD + 16 * TILES)
            sp.wait_ge(s["phase2_over"], 4)

            def load_y(t):
                if not is_first(t):
                    sp.wait_ge(s["yc_split"], HEAD + t)
                sp.dma_start(yc[:, :, :], y_scratch[:, :, bass.ds(t * TW, TW)]).then_inc(s["yc_loaded"], 16)

            def ffn_tile(t, more):
                if not is_first(t):
                    sp.wait_ge(s["out_ready"], HEAD + KD * t)
                sp.dma_start(resid2[:, :, :], x1_scratch[:, :, bass.ds(t * TW, TW)]).then_inc(s["resid2_loaded"], 16)
                if more:
                    load_y(t + 1)
                sp.wait_ge(s["out_ready"], HEAD + KD * (t + 1))
                sp.dma_start(out_t[:, :, bass.ds(t * TW, TW)], outs[:, :, :]).then_inc(s["out_stored"], 16)

            load_y(0)
            with sp.Fori(0, TILES - 1) as t:
                ffn_tile(t, True)
            ffn_tile(TILES - 1, False)
            sp.wait_ge(s["out_stored"], HEAD + 16 * TILES)

        @block.gpsimd
        def _(pool):
            for name in HEAD_STARTED:
                pool.sem_inc(s[name], HEAD)
            nc.gpsimd.memset(q_parts[:, :, :, :], 0.0).then_inc(s["const_made"], 1)
            nc.gpsimd.memset(m2[:, :, :, :], 0.0).then_inc(s["const_made"], 1)
            nc.gpsimd.memset(half[:, :], -0.5).then_inc(s["const_made"], 1)
            nc.gpsimd.memset(values_new[:, :, :], 0.0).then_inc(s["const_made"], 1)
            pool.wait_ge(s["const_made"], 4)
            nc.gpsimd.memset(values_new[:, :, HD:HD + 1], 1.0).then_inc(s["const_made"], 1)
            nc.gpsimd.memset(ones[:, :], 1.0).then_inc(s["const_made"], 1)
            pool.wait_ge(s["sel_loaded"], 16)
            nc.gpsimd.tensor_copy(sel[:, :], sel_raw[:, :]).then_inc(s["sel_made"], 1)
            pool.wait_ge(s["const_loaded"], 96)
            nc.gpsimd.tensor_copy(ident_b[:, :], ident[:, :]).then_inc(s["sel_made"], 1)

            def rstd_of(n):
                pool.wait_ge(s["veps_ready"], n + 1)
                if isinstance(n, int) and n == 0:
                    pool.wait_ge(s["const_made"], 6)
                nc.gpsimd.tensor_tensor(rstd[:, :], veps[:, :], half[:, :], ALU.pow).then_inc(s["rstd_ready"], 1)

            def high_again(n, t):
                pool.wait_ge(s["q_hi"], NT * n + t + 1)
                settle(pool, "pool_settled")
                nc.gpsimd.tensor_copy(q_parts[:, t, :, 2 * HD:3 * HD], q_parts[:, t, :, 0:HD]).then_inc(s["q_again"], 1)

            def split_fc():
                pool.wait_ge(s["raw_loaded"], 64)
                nc.gpsimd.tensor_copy(fc1_hi[:, :, :], fc1_raw.rearrange("p (k h) -> p k h", k=KD)).then_inc(s["split_step"], 1)
                nc.gpsimd.tensor_copy(fc2a_hi[:, :, :], fc2_raw[:, :, 0:P]).then_inc(s["split_step"], 1)
                for j in range(BT):
                    nc.gpsimd.tensor_copy(fc2b_hi[:, :, j, 0:SHARED - P], fc2_raw[:, :, P:SHARED]).then_inc(s["split_step"], 1)
                pool.wait_ge(s["split_step"], 2 + BT)
                nc.gpsimd.tensor_tensor(fc1_lo[:, :, :], fc1_raw.rearrange("p (k h) -> p k h", k=KD), fc1_hi[:, :, :].bitcast(F32), ALU.subtract).then_inc(s["fc_split"], 1)
                nc.gpsimd.tensor_tensor(fc2a_lo[:, :, :], fc2_raw[:, :, 0:P], fc2a_hi[:, :, :].bitcast(F32), ALU.subtract).then_inc(s["fc_split"], 1)
                for j in range(BT):
                    nc.gpsimd.tensor_tensor(fc2b_lo[:, :, j, 0:SHARED - P], fc2_raw[:, :, P:SHARED], fc2b_hi[:, :, j, 0:SHARED - P].bitcast(F32), ALU.subtract).then_inc(s["fc_split"], 1)

            rstd_of(0)
            high_again(0, 0)
            high_again(0, 1)
            split_fc()

            def move(b):
                pool.wait_ge(s["keys_low"], b + 1)
                pool.wait_ge(s["keys_out"], b + 1)
                if not is_first(b):
                    pool.wait_ge(s["score_mm"], FILLS * b)
                settle(pool, "pool_settled")
                nc.gpsimd.tensor_copy(keys[:, :], keys_new[:, :].bitcast(F32)).then_inc(s["keys_moved"], 1)
                pool.wait_ge(s["qv_out"], NT * (b + 1))
                if not is_first(b):
                    pool.wait_ge(s["late_mm"], b)
                settle(pool, "pool_settled")
                nc.gpsimd.tensor_copy(values[:, :, :], values_new[:, :, :]).then_inc(s["values_moved"], 1)

            def causal(b, f):
                pool.wait_ge(s["exp_done"], FILLS * b + f + 1)
                settle(pool, "pool_settled")
                first = score_fill(f)[0]
                v = p1[:, first // 4] if f in LATE else p0[:, first // 2]
                v = v.rearrange("p a c t -> p (a c) t")[:, :, 0:P]
                nc.gpsimd.affine_select(out=v, in_=v, compare_op=ALU.is_ge, fill=0.0, base=0,
                                        pattern=[[0, v.shape[1]], [1, P]], channel_multiplier=-1).then_inc(s["masked"], 1)

            def back(b, more):
                move(b)
                if more:
                    rstd_of(b + 1)
                    high_again(b + 1, 0)
                for f in range(FILLS):
                    causal(b, f)
                if more:
                    high_again(b + 1, 1)

            back(0, True)
            with pool.Fori(1, B - 1) as b:
                back(b, True)
            back(B - 1, False)
            pool.wait_ge(s["fc_split"], 2 + BT)
            pool.wait_ge(s["masked"], FILLS * B)
            pool.sem_inc(s["phase1_over"], 1)
            pool.wait_ge(s["phase1_over"], 4)

            with pool.Fori(0, TILES) as t:
                pool.wait_ge(s["expert_loaded"], 16 * BT * (t + 1))
                pool.wait_ge(s["unit_mm"], HEAD + (KH + KD) * t)
                settle(pool, "pool_settled")
                for j in range(BT):
                    nc.gpsimd.tensor_copy(fc2b_hi[:, :, j, SHARED - P:P], exp_raw[:, j]).then_inc(s["expert_hi"], 1)
                pool.wait_ge(s["expert_hi"], BT * (t + 1))
                for j in range(BT):
                    nc.gpsimd.tensor_tensor(fc2b_lo[:, :, j, SHARED - P:P], exp_raw[:, j], fc2b_hi[:, :, j, SHARED - P:P].bitcast(F32), ALU.subtract).then_inc(s["expert_split"], 1)
            pool.wait_ge(s["expert_split"], HEAD + BT * TILES)
            pool.sem_inc(s["phase2_over"], 1)

        @block.scalar
        def _(act):
            def hidden(n):
                act.wait_ge(s["hidden_mm"], n + 1)
                nc.scalar.activation(h_t[0:A, :], side[0][0:A, 0:T], ACT.Relu, bias=vec[0:A, 4:5]).then_inc(s["hidden_out"], 1)

            def affine(n):
                act.wait_ge(s["norm_t_mm"], n + 1)
                for k in range(KD):
                    last = nc.scalar.activation(norm_t[:, k, :], side[1][:, k * T:(k + 1) * T], ACT.Identity,
                                                bias=vec[:, 2 + k:3 + k], scale=vec[:, k:k + 1])
                last.then_inc(s["norm_t_out"], 1)

            def queries_out(b, t):
                act.wait_ge(s["q_t_mm"], 4 * b + 2 * t + 1)
                nc.scalar.activation(q_t[:, 0:4, t * P:(t + 1) * P], ring[0][:, :].rearrange("p (c t) -> p c t", c=4),
                                     ACT.Copy).then_inc(s["q_t_act"], 1)

            def exponential(b, f):
                act.wait_ge(s["score_mm"], FILLS * b + f + 1)
                first = score_fill(f)[0]
                dst = p1[:, first // 4] if f in LATE else p0[:, first // 2]
                nc.scalar.activation(dst.rearrange("p a c t -> p a (c t)"), pair_bank[f % 2][:, :, :], ACT.Exp).then_inc(s["exp_done"], 1)

            def attention_out(b):
                act.wait_ge(s["att_t_mm"], b + 1)
                nc.scalar.activation(att_t[:, :, :], side[0][:, :].rearrange("p (k t) -> p k t", k=KD), ACT.Copy).then_inc(s["att_t_out"], 1)

            def back(b, prev, more):
                queries_out(b, 0)
                queries_out(b, 1)
                if more:
                    hidden(b + 1)
                if prev:
                    attention_out(b - 1)
                if more:
                    affine(b + 1)
                act.wait_ge(s["max_t_mm"], b + 1)
                nc.scalar.activation(m_t[:, :], side[1][:, 0:T], ACT.Copy).then_inc(s["max_t_out"], 1)
                for f in range(4):
                    exponential(b, f)
                act.wait_ge(s["early_mm"], b + 1)
                nc.scalar.activation(pv[:, 0:2, :], ring[1][:, :].rearrange("p (g t) -> p g t", g=2), ACT.Copy).then_inc(s["early_out"], 1)
                for f in range(4, 6):
                    exponential(b, f)

            act.wait_ge(s["front_loaded"], 80)
            hidden(0)
            affine(0)
            act.wait_ge(s["fc_split"], 2 + BT)
            back(0, False, True)
            with act.Fori(1, B - 1) as b:
                back(b, True, True)
            back(B - 1, True, False)
            attention_out(B - 1)
            act.wait_ge(s["att_t_out"], B)
            act.sem_inc(s["phase1_over"], 1)
            act.wait_ge(s["phase1_over"], 4)

            with act.Fori(0, TILES) as t:
                for m in range(KH):
                    act.wait_ge(s["unit_mm"], HEAD + (KH + KD) * t + m + 1)
                    if m >= 2:
                        act.wait_ge(s["act_ready"], HEAD + KH * t + m - 1)
                    else:
                        act.wait_ge(s["act_ready"], HEAD + KH * t)
                    nc.scalar.activation(g_raw[:, m % 2, :], banks[m % 6], ACT.Gelu, bias=fc1_bias[:, m:m + 1]).then_inc(s["raw_ready"], 1)
            act.wait_ge(s["raw_ready"], KH * TILES)
            act.sem_inc(s["phase2_over"], 1)
            act.wait_ge(s["phase2_over"], 4)

            with act.Fori(0, TILES) as t:
                for m in range(KH):
                    act.wait_ge(s["c_mm"], C_UNITS * t + 2 * m + 1)
                    if m >= 2:
                        act.wait_ge(s["prod_ready"], HEAD + KH * t + m - 1)
                    else:
                        act.wait_ge(s["prod_ready"], HEAD + KH * t)
                    nc.scalar.activation(sil[:, m % 2, :], banks[(2 * m) % 8], ACT.Silu, scale=SC_W1[:, m:m + 1]).then_inc(s["sil_ready"], 1)
                for layer in range(2):
                    for m in range(KH):
                        g = 2 * KH + layer * KH + m
                        act.wait_ge(s["c_mm"], C_UNITS * t + g + 1)
                        act.wait_ge(s["c_ready"], 3 * KH * t + (1 + layer) * KH + m - 1)
                        sc = (SC_H1, SC_H2)[layer]
                        nc.scalar.activation(h_raw[:, m % 2, :], banks[g % 8], ACT.Gelu, scale=sc[:, m:m + 1]).then_inc(s["c_act"], 1)

        @block.vector
        def _(dve):
            def add_adapted(n):
                dve.wait_ge(s["adapted_mm"], n + 1)
                nc.vector.tensor_tensor(u[:, :, :], side[1][:, :].rearrange("p (t d) -> p t d", t=NT), xtok[:, :, :], ALU.add).then_inc(s["u_out"], 1)
                dve.wait_ge(s["u_out"], n + 1)
                for t in range(NT):
                    nc.vector.bn_stats(stats[:, t, :], u[:, t, :]).then_inc(s["stats_ready"], 1)
                dve.wait_ge(s["stats_ready"], NT * (n + 1))
                settle(dve, "dve_settled")
                for t in range(NT):
                    nc.vector.bn_aggr(moments[:, t, :], stats[:, t, :]).then_inc(s["moments_ready"], 1)
                dve.wait_ge(s["moments_ready"], NT * (n + 1))
                nc.vector.tensor_scalar(veps[:, :], moments[:, :, 1], EPS, None, ALU.add).then_inc(s["veps_ready"], 1)

            def normalise(n):
                dve.wait_ge(s["rstd_ready"], n + 1)
                for t in range(NT):
                    nc.vector.tensor_scalar(norm[:, t, :], u[:, t, :], moments[:, t, 0:1], rstd[:, t:t + 1],
                                            ALU.subtract, ALU.mult).then_inc(s["norm_ready"], 1)

            def keys_of(n):
                dve.wait_ge(s["keys_mm"], n + 1)
                if not is_first(n):
                    dve.wait_ge(s["keys_moved"], n)
                src = side[0]
                nc.vector.tensor_copy(keys_new[:, :], src[:, 0:T]).then_inc(s["keys_hi"], 1)
                dve.wait_ge(s["keys_hi"], n + 1)
                nc.vector.tensor_tensor(keys_new[32:64, :], src[32:64, 0:T], keys_new[32:64, :].bitcast(F32), ALU.subtract).then_inc(s["keys_low"], 1)
                nc.vector.tensor_tensor(keys_new[96:128, :], src[96:128, 0:T], keys_new[96:128, :].bitcast(F32), ALU.subtract).then_inc(s["keys_out"], 1)

            def queries_of(n, t):
                dve.wait_ge(s["qv_mm"], NT * n + t + 1)
                if not is_first(n):
                    dve.wait_ge(s["values_moved"], n)
                src = side[t]
                q = src[:, 0:D].rearrange("p (h c) -> p h c", h=NH)
                nc.vector.tensor_scalar(q_parts[:, t, :, 0:HD].bitcast(F32R), q, QSCALE, None, ALU.mult).then_inc(s["q_hi"], 1)
                dve.wait_ge(s["q_hi"], NT * n + t + 1)
                nc.vector.scalar_tensor_tensor(out=q_parts[:, t, :, HD:2 * HD].bitcast(F32R), in0=q, scalar=QSCALE, in1=q_parts[:, t, :, 0:HD],
                                               op0=ALU.mult, op1=ALU.subtract).then_inc(s["q_low"], 1)
                nc.vector.tensor_copy(values_new[:, t, 0:HD], src[:, D:D + HD]).then_inc(s["qv_out"], 1)

            def queries_out(b, t):
                dve.wait_ge(s["q_t_mm"], 4 * b + 2 * t + 2)
                nc.vector.tensor_copy(q_t[:, 4:8, t * P:(t + 1) * P], ring[1][:, :].rearrange("p (c t) -> p c t", c=4)).then_inc(s["q_t_dve"], 1)

            def maximum(b, f):
                dve.wait_ge(s["max_mm"], FILLS * b + f + 1)
                t, first, pairs = max_fill(f)
                nc.vector.tensor_reduce(neg_max[:, t, first:first + pairs, :].rearrange("p c a -> p a c"),
                                        pair_bank[f % 2][:, :, :].rearrange("p a (c k) -> p a c k", c=pairs),
                                        AX.X, ALU.max, negate=True).then_inc(s["max_out"], 1)

            def split_maxima(b):
                dve.wait_ge(s["max_out"], FILLS * (b + 1))
                nm = neg_max[:, :, :, :].rearrange("p t c a -> p t (c a)")
                for half_ in range(2):
                    nc.vector.tensor_copy(m2[:, :, half_, 0:NH].bitcast(F32R), nm).then_inc(s["m2_hi"], 1)
                dve.wait_ge(s["m2_hi"], 2 * (b + 1))
                for half_ in range(2):
                    nc.vector.tensor_tensor(m2[:, :, half_, NH:2 * NH].bitcast(F32R), nm, m2[:, :, half_, 0:NH], ALU.subtract).then_inc(s["m2_ready"], 1)

            def attention(b, t):
                dve.wait_ge(s["pv_t_mm"], NT * b + t + 1)
                o = side[1 - t][:, :].rearrange("p (h c) -> p h c", h=NH)
                nc.vector.reciprocal(recip[:, t, :], o[:, :, HD]).then_inc(s["recip_done"], 1)
                dve.wait_ge(s["recip_done"], NT * b + t + 1)
                nc.vector.tensor_tensor(att[:, t, :].rearrange("p (h c) -> p h c", h=NH), o[:, :, 0:HD],
                                        recip[:, t, :].rearrange("p (h c) -> p h c", c=1).broadcast_to([P, NH, HD]), ALU.mult).then_inc(s["att_out"], 1)

            def add_residual(b):
                dve.wait_ge(s["resid_loaded"], 16 * (b + 1))
                if not is_first(b):
                    dve.wait_ge(s["x1_stored"], 16 * b)
                for m in range(KD):
                    dve.wait_ge(s["proj_mm"], KD * b + m + 1)
                    nc.vector.scalar_tensor_tensor(out=x1[:, m, :], in0=side[1 - m][:, 0:T], scalar=bf[:, m:m + 1], in1=resid[:, m, :],
                                                   op0=ALU.add, op1=ALU.add).then_inc(s["x1_out"], 1)

            def back(b, prev, more):
                queries_out(b, 0)
                queries_out(b, 1)
                maximum(b, 0)
                if prev:
                    attention(b - 1, 0)
                    attention(b - 1, 1)
                maximum(b, 1)
                if more:
                    add_adapted(b + 1)
                maximum(b, 2)
                if more:
                    normalise(b + 1)
                maximum(b, 3)
                if prev:
                    add_residual(b - 1)
                maximum(b, 4)
                maximum(b, 5)
                split_maxima(b)
                if more:
                    keys_of(b + 1)
                    queries_of(b + 1, 0)
                    queries_of(b + 1, 1)
                dve.wait_ge(s["late_mm"], b + 1)
                nc.vector.tensor_copy(pv[:, 2:4, :], ring[0][:, :].rearrange("p (g t) -> p g t", g=2)).then_inc(s["late_out"], 1)

            nc.vector.memset(h_t[A:A + 1, :], 1.0).then_inc(s["row_made"], 1)
            dve.wait_ge(s["front_loaded"], 80)
            dve.wait_ge(s["const_made"], 6)
            dve.wait_ge(s["const_loaded"], 96)
            add_adapted(0)
            normalise(0)
            keys_of(0)
            queries_of(0, 0)
            queries_of(0, 1)
            back(0, False, True)
            with dve.Fori(1, B - 1) as b:
                back(b, True, True)
            back(B - 1, True, False)
            attention(B - 1, 0)
            attention(B - 1, 1)
            add_residual(B - 1)
            dve.wait_ge(s["x1_out"], KD * B)
            dve.sem_inc(s["phase1_over"], 1)
            dve.wait_ge(s["phase1_over"], 4)

            nc.vector.memset(bits[:, :], 0.0).then_inc(s["bits_step"], 1)
            dve.wait_ge(s["ffn_loaded"], 16)
            def split_x(t):
                dve.wait_ge(s["xa_loaded"], 16 * (t + 1))
                if not is_first(t):
                    dve.wait_ge(s["unit_mm"], HEAD + (KH + KD) * (t - 1) + KH)
                nc.vector.tensor_copy(xa_hi[:, :, :], xa[:, :, :]).then_inc(s["xa_hi"], 1)
                dve.wait_ge(s["xa_hi"], t + 1)
                nc.vector.tensor_tensor(xa_lo[:, :, :], xa[:, :, :], xa_hi[:, :, :].bitcast(F32), ALU.subtract).then_inc(s["xa_split"], 1)

            def cond2_tile(t, more):
                for m in range(KH):
                    dve.wait_ge(s["raw_ready"], KH * t + m + 1)
                    nc.vector.tensor_copy(g_hi[:, m, :], g_raw[:, m % 2, :]).then_inc(s["hi_ready"], 1)
                    dve.wait_ge(s["hi_ready"], KH * t + m + 1)
                    nc.vector.tensor_tensor(g_lo[:, m, :], g_raw[:, m % 2, :], g_hi[:, m, :].bitcast(F32), ALU.subtract).then_inc(s["act_ready"], 1)
                if more:
                    split_x(t + 1)
                dve.wait_ge(s["bits_step"], t + 1)
                nc.vector.tensor_tensor(bits[:, :], bits[:, :], ffn_w[:, bass.ds(t * CHECK, CHECK)].bitcast(U32), ALU.bitwise_or).then_inc(s["bits_step"], 1)
                dve.wait_ge(s["bias_loaded"], 16 * (1 + BT) + 16 * BT * (t + 1))
                if not is_first(t):
                    dve.wait_ge(s["y_stored"], HEAD + 16 * t)
                dve.wait_ge(s["unit_mm"], HEAD + (KH + KD) * t + KH + 1)
                nc.vector.tensor_scalar(y[:, 0, :], banks[6], fc2_bias[:, 0:1], None, ALU.add).then_inc(s["y_ready"], 1)
                dve.wait_ge(s["unit_mm"], HEAD + (KH + KD) * t + KH + 2)
                for j in range(BT):
                    nc.vector.tensor_scalar(y[:, 1, j * T:(j + 1) * T], banks[7][:, j * T:(j + 1) * T], fc2_bias[:, 1 + j:2 + j], None, ALU.add).then_inc(s["y_ready"], 1)

            split_x(0)
            with dve.Fori(0, TILES - 1) as t:
                cond2_tile(t, True)
            cond2_tile(TILES - 1, False)
            dve.wait_ge(s["bits_step"], TILES + 1)
            nc.vector.tensor_scalar(bits_low[:, :], bits[:, :], 0xFFF, None, ALU.bitwise_and).then_inc(s["bits_step"], 1)
            dve.wait_ge(s["bits_step"], TILES + 2)
            nc.vector.tensor_reduce(bits_top[:, :], bits_low[:, :], AX.X, ALU.max).then_inc(s["bits_step"], 1)
            dve.wait_ge(s["bits_step"], TILES + 3)
            nc.vector.tensor_copy(low_bits[:, :], bits_top[:, :]).then_inc(s["bits_max"], 1)
            dve.wait_ge(s["bits_summed"], 1)
            nc.vector.tensor_copy(low_count[:, :], bank[2][0:1, 0:1]).then_inc(s["flag_ready"], 1)
            dve.wait_ge(s["y_ready"], HEAD + 3 * TILES)
            dve.wait_ge(s["flag_ready"], 1)
            dve.sem_inc(s["phase2_over"], 1)
            dve.wait_ge(s["phase2_over"], 4)

            def split(dst_hi, dst_lo, src, done):
                nc.vector.tensor_copy(dst_hi, src).then_inc(s["c_hi"], 1)
                dve.wait_ge(s["c_hi"], done + 1)
                nc.vector.tensor_tensor(dst_lo, src, dst_hi.bitcast(F32), ALU.subtract).then_inc(s["c_ready"], 1)

            def split_y(t):
                dve.wait_ge(s["yc_loaded"], 16 * (t + 1))
                if not is_first(t):
                    dve.wait_ge(s["c_mm"], C_UNITS * (t - 1) + 2 * KH)
                nc.vector.tensor_copy(yc_hi[:, :, :], yc[:, :, :]).then_inc(s["yc_hi"], 1)
                dve.wait_ge(s["yc_hi"], t + 1)
                nc.vector.tensor_tensor(yc_lo[:, :, :], yc[:, :, :], yc_hi[:, :, :].bitcast(F32), ALU.subtract).then_inc(s["yc_split"], 1)

            def ffn_tile(t, more):
                for m in range(KH):
                    dve.wait_ge(s["sil_ready"], KH * t + m + 1)
                    dve.wait_ge(s["c_mm"], C_UNITS * t + 2 * m + 2)
                    if m < 2 and not is_first(t):
                        dve.wait_ge(s["c_ready"], 3 * KH * t)
                    nc.vector.scalar_tensor_tensor(out=h_raw[:, m % 2, :], in0=banks[(2 * m + 1) % 8], scalar=SC_W2[:, m:m + 1],
                                                   in1=sil[:, m % 2, :], op0=ALU.mult, op1=ALU.mult).then_inc(s["prod_ready"], 1)
                    dve.wait_ge(s["prod_ready"], HEAD + KH * t + m + 1)
                    split(h_hi[0][:, m, :], h_lo[0][:, m, :], h_raw[:, m % 2, :], 3 * KH * t + m)
                for layer in range(2):
                    for m in range(KH):
                        dve.wait_ge(s["c_act"], HEAD + 2 * KH * t + layer * KH + m + 1)
                        split(h_hi[1 - layer][:, m, :], h_lo[1 - layer][:, m, :], h_raw[:, m % 2, :], 3 * KH * t + (1 + layer) * KH + m)
                    if layer == 0 and more:
                        split_y(t + 1)
                dve.wait_ge(s["resid2_loaded"], 16 * (t + 1))
                if not is_first(t):
                    dve.wait_ge(s["out_stored"], HEAD + 16 * t)
                for m in range(KD):
                    dve.wait_ge(s["c_mm"], C_UNITS * t + 4 * KH + m + 1)
                    nc.vector.scalar_tensor_tensor(out=outs[:, m, :], in0=banks[6 + m], scalar=SC_W3[:, m:m + 1], in1=resid2[:, m, :],
                                                   op0=ALU.mult, op1=ALU.add).then_inc(s["out_ready"], 1)

            split_y(0)
            with dve.Fori(0, TILES - 1) as t:
                ffn_tile(t, True)
            ffn_tile(TILES - 1, False)

        @block.tensor
        def _(pe):
            mm = nc.tensor.matmul

            def half_rows(par):
                return slice(SLOT * par, SLOT * (par + 1))

            def adapter_in(n):
                pe.wait_ge(s["front_loaded"], 80 * (n + 1))
                if not is_first(n):
                    pe.wait_ge(s["qv_out"], NT * (n - 1) + 1)
                for k in range(KD):
                    last = mm(side[0][0:A, 0:T], w1c[:, k, :], xt[:, k, :], start=k == 0, stop=k == KD - 1)
                last.then_inc(s["hidden_mm"], 1)

            def adapter_out(n, prev):
                pe.wait_ge(s["hidden_out"], n + 1)
                if prev:
                    pe.wait_ge(s["att_out"], NT * (n - 2) + 1)
                elif not is_first(n):
                    pe.wait_ge(s["qv_out"], NT * n)
                for t in range(NT):
                    last = mm(side[1][:, t * D:(t + 1) * D], h_t[:, t * P:(t + 1) * P], w2c[:, :], start=True, stop=True)
                last.then_inc(s["adapted_mm"], 1)

            def norm_transposed(n, prev):
                pe.wait_ge(s["norm_ready"], NT * (n + 1))
                if prev:
                    pe.wait_ge(s["x1_out"], KD * (n - 2) + 1)
                for k in range(KD):
                    for t in range(NT):
                        last = nc.tensor.transpose(side[1][:, k * T + t * P:k * T + (t + 1) * P], norm[:, t, k * P:(k + 1) * P], ident[:, :])
                last.then_inc(s["norm_t_mm"], 1)

            def project_keys(n, prev):
                pe.wait_ge(s["norm_t_out"], n + 1)
                if prev:
                    pe.wait_ge(s["x1_out"], KD * (n - 1))
                for k in range(KD):
                    last = mm(side[0][:, 0:T], wk[:, k, :], norm_t[:, k, :], start=k == 0, stop=k == KD - 1)
                last.then_inc(s["keys_mm"], 1)

            def project_queries(n, t):
                if t == 0:
                    pe.wait_ge(s["keys_out"], n + 1)
                elif not is_first(n):
                    pe.wait_ge(s["max_t_out"], n)
                for k in range(KD):
                    last = mm(side[t][:, 0:D + HD], norm_t[:, k, t * P:(t + 1) * P], wqv[:, k, :], start=k == 0, stop=k == KD - 1)
                last.then_inc(s["qv_mm"], 1)

            def queries_transposed(b, t, j):
                pe.wait_ge(s["q_low"], NT * b + t + 1)
                pe.wait_ge(s["q_again"], NT * b + t + 1)
                if t == 1:
                    pe.wait_ge(s["q_t_dve" if j else "q_t_act"], NT * b + 1)
                elif not is_first(b):
                    pe.wait_ge(s["early_out" if j else "late_out"], b)
                for c in range(4):
                    pair = 4 * j + c
                    last = nc.tensor.transpose(ring[j][:, c * P:(c + 1) * P], q_parts[:, t, 2 * pair:2 * pair + 2, :], ident[:, :])
                last.then_inc(s["q_t_mm"], 1)

            def max_scores(b, f):
                t, first, pairs = max_fill(f)
                if f in (0, 2):
                    pe.wait_ge(s["q_t_act"], NT * b + t + 1)
                    pe.wait_ge(s["q_t_dve"], NT * b + t + 1)
                if f == 0:
                    pe.wait_ge(s["keys_moved"], b + 1)
                if f >= 2:
                    pe.wait_ge(s["max_out"], FILLS * b + f - 1)
                elif not is_first(b):
                    pe.wait_ge(s["exp_done"], FILLS * b + f - 1)
                n = P * (t + 1)
                for c in range(pairs):
                    for par in range(2):
                        r = half_rows(par)
                        mm(pair_bank[f % 2][:, par, c * n:(c + 1) * n], q_t[r, first + c, t * P:(t + 1) * P], keys[r, 0:n], start=c == 0, stop=False)
                for par in range(2):
                    diag = pair_bank[f % 2][:, par, :].rearrange("p (h k) -> p h k", h=pairs)[:, :, n - P:n]
                    last = mm(diag, ident_b[:, :], mask[:, 0:pairs, :], start=False, stop=True)
                last.then_inc(s["max_mm"], 1)

            def maxima_transposed(b, prev, more):
                pe.wait_ge(s["m2_ready"], 2 * (b + 1))
                if not more:
                    pe.wait_ge(s["x1_out"], KD * (b - 1) + 1)
                for t in range(NT):
                    last = nc.tensor.transpose(side[1][:, t * P:(t + 1) * P], m2[:, t, :, :].rearrange("p a c -> p (a c)"), ident[:, :])
                last.then_inc(s["max_t_mm"], 1)

            def scores(b, f):
                if f == 0:
                    pe.wait_ge(s["max_t_out"], b + 1)
                if f >= 2:
                    pe.wait_ge(s["exp_done"], FILLS * b + f - 1)
                else:
                    pe.wait_ge(s["max_out"], FILLS * b + 5 + f)
                first, pairs, k0, q0 = score_fill(f)
                n = T - q0
                for par in range(2):
                    r = half_rows(par)
                    mm(pair_bank[f % 2][:, par, :].rearrange("p (c t) -> p c t", c=pairs), keys[r, k0:k0 + P], q_t[r, first:first + pairs, q0:T],
                       start=True, stop=False)
                for c in range(pairs):
                    for par in range(2):
                        r = half_rows(par)
                        h = 2 * (first + c) + par
                        last = mm(pair_bank[f % 2][:, par, c * n:(c + 1) * n], sel[r, h:h + 1].broadcast_to([SLOT, P]), m_t[r, q0:T],
                                  start=False, stop=c == pairs - 1)
                last.then_inc(s["score_mm"], 1)

            def products(b, late):
                pe.wait_ge(s["masked"], FILLS * b + (6 if late else 3))
                if not late:
                    pe.wait_ge(s["values_moved"], b + 1)
                dst = ring[0 if late else 1]
                for g in (2, 3) if late else (0, 1):
                    at = (g % 2) * T
                    for key_tile in range(NT):
                        for j in range(4):
                            c, par = j // 2, j % 2
                            rows = slice(32 * j, 32 * (j + 1))
                            if key_tile == 0:
                                last = mm(dst[rows, at:at + T], values[:, 0, :], p0[:, g, par, c, :], start=True, stop=False)
                            else:
                                last = mm(dst[rows, at + P:at + T], values[:, 1, :], p1[:, g // 2, par, 2 * (g % 2) + c, :],
                                          start=False, stop=True)
                last.then_inc(s["late_mm" if late else "early_mm"], 1)

            def products_transposed(b, t, more):
                if t == 0:
                    pe.wait_ge(s["early_out"], b + 1)
                    pe.wait_ge(s["late_out"], b + 1)
                    if is_last(b):
                        pe.wait_ge(s["max_t_out"], B)
                    else:
                        pe.wait_ge(s["qv_out"], NT * (b + 2))
                elif is_last(b):
                    pe.wait_ge(s["x1_out"], KD * (B - 1))
                elif more:
                    pe.wait_ge(s["hidden_out"], b + 3)
                for g in range(4):
                    last = nc.tensor.transpose(side[1 - t][:, g * P:(g + 1) * P], pv[:, g, t * P:(t + 1) * P], ident[:, :])
                last.then_inc(s["pv_t_mm"], 1)

            def attention_transposed(b):
                pe.wait_ge(s["att_out"], NT * (b + 1))
                for k in range(KD):
                    for t in range(NT):
                        last = nc.tensor.transpose(side[0][:, k * T + t * P:k * T + (t + 1) * P], att[:, t, k * P:(k + 1) * P], ident[:, :])
                last.then_inc(s["att_t_mm"], 1)

            def project_out(b, more):
                pe.wait_ge(s["att_t_out"], b + 1)
                if more:
                    pe.wait_ge(s["u_out"], b + 3)
                for m in range(KD):
                    for k in range(KD):
                        last = mm(side[1 - m][:, 0:T], wf[:, k, m * P:(m + 1) * P], att_t[:, k, :], start=k == 0, stop=k == KD - 1)
                    last.then_inc(s["proj_mm"], 1)

            def back(b, prev, more):
                queries_transposed(b, 0, 0)
                queries_transposed(b, 0, 1)
                if more:
                    adapter_in(b + 1)
                queries_transposed(b, 1, 0)
                queries_transposed(b, 1, 1)
                max_scores(b, 0)
                if prev:
                    products_transposed(b - 1, 0, more)
                    products_transposed(b - 1, 1, more)
                max_scores(b, 1)
                if more:
                    adapter_out(b + 1, prev)
                max_scores(b, 2)
                if prev:
                    attention_transposed(b - 1)
                max_scores(b, 3)
                if prev:
                    project_out(b - 1, more)
                max_scores(b, 4)
                if more:
                    norm_transposed(b + 1, prev)
                max_scores(b, 5)
                if more:
                    project_keys(b + 1, prev)
                maxima_transposed(b, prev, more)
                if more:
                    project_queries(b + 1, 0)
                for f in range(4):
                    scores(b, f)
                products(b, False)
                for f in range(4, 6):
                    scores(b, f)
                if more:
                    project_queries(b + 1, 1)
                products(b, True)

            pe.wait_ge(s["const_loaded"], 96)
            pe.wait_ge(s["const_made"], 6)
            pe.wait_ge(s["sel_made"], 2)
            pe.wait_ge(s["row_made"], 1)
            adapter_in(0)
            adapter_out(0, False)
            norm_transposed(0, False)
            project_keys(0, False)
            project_queries(0, 0)
            project_queries(0, 1)
            back(0, False, True)
            with pe.Fori(1, B - 1) as b:
                back(b, True, True)
            back(B - 1, True, False)
            products_transposed(B - 1, 0, False)
            products_transposed(B - 1, 1, False)
            attention_transposed(B - 1)
            project_out(B - 1, False)
            pe.wait_ge(s["late_mm"], B)
            pe.wait_ge(s["proj_mm"], KD * B)
            pe.sem_inc(s["phase1_over"], 1)
            pe.wait_ge(s["phase1_over"], 4)

            with pe.Fori(0, TILES) as t:
                pe.wait_ge(s["xa_split"], HEAD + t + 1)
                for m in range(KH):
                    if m >= 6:
                        pe.wait_ge(s["raw_ready"], KH * t + m - 5)
                    cols = slice(m * P, (m + 1) * P)
                    passes = [(w, v, k) for w, v in ((fc1_hi, xa_hi), (fc1_hi, xa_lo), (fc1_lo, xa_hi)) for k in range(KD)]
                    for i, (w, v, k) in enumerate(passes):
                        last = mm(banks[m % 6], w[:, k, cols], v[:, k, :], start=i == 0, stop=i == len(passes) - 1)
                    last.then_inc(s["unit_mm"], 1)
                pe.wait_ge(s["y_ready"], HEAD + (1 + BT) * t)
                for k in range(KH):
                    pe.wait_ge(s["act_ready"], HEAD + KH * t + k + 1)
                    for i, (w, v) in enumerate(((fc2a_hi, g_hi), (fc2a_hi, g_lo), (fc2a_lo, g_hi))):
                        last = mm(banks[6], w[:, k, :], v[:, k, :], start=k == 0 and i == 0, stop=k == KH - 1 and i == 2)
                last.then_inc(s["unit_mm"], 1)
                pe.wait_ge(s["expert_split"], HEAD + BT * (t + 1))
                for j in range(BT):
                    for k in range(KH):
                        for i, (w, v) in enumerate(((fc2b_hi, g_hi), (fc2b_hi, g_lo), (fc2b_lo, g_hi))):
                            last = mm(banks[7][:, j * T:(j + 1) * T], w[:, k, j, :], v[:, k, j * T:(j + 1) * T],
                                      start=k == 0 and i == 0, stop=k == KH - 1 and i == 2)
                last.then_inc(s["unit_mm"], 1)
            pe.wait_ge(s["bits_max"], 1)
            mm(bank[2][0:1, 0:1], low_bits[:, :], ones[:, :], start=True, stop=True).then_inc(s["bits_summed"], 1)
            pe.wait_ge(s["flag_ready"], 1)
            pe.sem_inc(s["phase2_over"], 1)
            pe.wait_ge(s["phase2_over"], 4)

            def ffn(dt):
                def w_at(at, k, width, m):
                    w = ffn_w[:, at + k * width + m * P:at + k * width + (m + 1) * P]
                    return w if dt is F32R else w.bitcast(dt)

                def v_at(v, k):
                    return v[:, k, :] if dt is F32R else v[:, k, :].bitcast(dt)

                def unit(t, bank, at, width, m, hi, lo, tiles, ready):
                    for k in range(tiles):
                        if ready is not None and m == 0:
                            pe.wait_ge(s["c_ready"], ready + k + 1)
                        for i, v in enumerate((hi, lo)):
                            last = mm(bank, w_at(at, k, width, m), v_at(v, k), start=k == 0 and i == 0, stop=k == tiles - 1 and i == 1)
                    last.then_inc(s["c_mm"], 1)

                with pe.Fori(0, TILES) as t:
                    pe.wait_ge(s["yc_split"], HEAD + t + 1)
                    for m in range(KH):
                        if m >= 4:
                            pe.wait_ge(s["sil_ready"], KH * t + m - 3)
                        elif m == 3:
                            pe.wait_ge(s["out_ready"], HEAD + KD * t)
                        unit(t, banks[(2 * m) % 8], W1_AT, HID, m, yc_hi, yc_lo, KD, None)
                        if m >= 4:
                            pe.wait_ge(s["prod_ready"], HEAD + KH * t + m - 3)
                        unit(t, banks[(2 * m + 1) % 8], W2_AT, HID, m, yc_hi, yc_lo, KD, None)
                    for layer, at in enumerate((H1_AT, H2_AT)):
                        for m in range(KH):
                            if layer == 0:
                                pe.wait_ge(s["prod_ready"], HEAD + KH * t + 5 + m // 2)
                            else:
                                pe.wait_ge(s["c_act"], HEAD + 2 * KH * t + m + 1)
                            unit(t, banks[m], at, HID, m, h_hi[layer], h_lo[layer], KH, 3 * KH * t + layer * KH)
                    for m in range(KD):
                        pe.wait_ge(s["c_act"], HEAD + 2 * KH * t + KH + 6 + m + 1)
                        unit(t, banks[6 + m], W3_AT, D, m, h_hi[0], h_lo[0], KH, 3 * KH * t + 2 * KH)

            with pe.register("low_bits_found") as found:
                nc.tensor.reg_load(found, low_count[0:1, 0:1])
                with pe.If_ne(found, 0):
                    ffn(F32)
                with pe.Else():
                    ffn(F32R)


def tiles(a):
    a = np.ascontiguousarray(a)
    return np.ascontiguousarray(a.reshape(-1, P, a.shape[-1]).transpose(1, 0, 2))


def kernel(**inputs):
    import ml_dtypes
    import concourse.bacc as _bacc
    from concourse.bass_utils import run_bass_kernel_spmd as _run

    g = {k: np.asarray(v) for k, v in inputs.items()}
    z = np.zeros
    x = g["x"]
    a = {}
    a["x_t"] = tiles(x.reshape(TOK, D).T)
    a["x_tok"] = x.reshape(B, NT, P, D).transpose(0, 2, 1, 3)
    a["lang"] = g["itok_B_0_8"].reshape(1, B)
    a["expert"] = g["itok_B_0_15"].reshape(1, B)
    a["cond_w1"] = g["L0_cond_W1"].reshape(L, KD, P, A).transpose(0, 2, 1, 3)
    a["cond_w2"] = np.concatenate([g["L0_cond_W2"], g["L0_cond_b2"][:, None, :]], 1)
    vec = z((L, P, 5), np.float32)
    vec[:, :, 0:2] = g["L0_cond_gamma"].reshape(L, KD, P).transpose(0, 2, 1)
    vec[:, :, 2:4] = g["L0_cond_beta"].reshape(L, KD, P).transpose(0, 2, 1)
    vec[:, 0:A, 4] = g["L0_cond_b1"]
    a["cond_vec"] = vec
    a["w_qv"] = tiles(np.concatenate([g["L0_attn_Wq"].T, g["L0_attn_Wv"].T], 1))
    wk = z((D, P), np.float32)
    for at in (0, 16, 32, 64, 80, 96):
        wk[:, at:at + HD] = g["L0_attn_Wk"].T
    a["w_k"] = tiles(wk)
    a["w_f"] = tiles(g["L0_attn_Wf"].T)
    a["b_f"] = g["L0_attn_bf"].reshape(KD, P).T
    a["ident_d"] = np.eye(P, dtype=np.float32)
    q, k = np.arange(P)[:, None, None], np.arange(P)[None, None, :]
    a["mask_d"] = np.broadcast_to(np.where(k > q, -1e30, 0.0), (P, 4, P)).astype(ml_dtypes.bfloat16)
    sel = z((P, NH), np.float32)
    for h in range(NH):
        sel[[h, h + NH, h + SLOT, h + SLOT + NH], h] = 1.0
    a["sel_d"] = sel
    a["fc1_w"] = tiles(g["L0_cond2_fc1_w"].T).reshape(P, KD * HID)
    a["fc1_b"] = g["L0_cond2_fc1_b"].reshape(KH, P).T
    a["fc2_w"] = tiles(g["L0_cond2_fc2_w"].T)
    fc2_b = z((2, P, 1), np.float32)
    fc2_b.reshape(-1)[0:SHARED] = g["L0_cond2_fc2_b"]
    a["fc2_b"] = fc2_b
    a["exp_w"] = g["L0_cond2_experts_w"].reshape(E, PART, KH, P).transpose(0, 3, 2, 1)
    a["exp_b"] = g["L0_cond2_experts_b"].reshape(E, PART, 1)
    a["ffn_d"] = np.concatenate([tiles(g[f"L0_ffn_{n}_w"].T).reshape(P, -1) for n in ("w1", "w2", "h1", "h2", "w3")], 1)
    a["ffn_s"] = np.concatenate([g[f"L0_ffn_{n}_s"].reshape(-1, P).T for n in ("w1", "w2", "h1", "h2", "w3")], 1)

    nc = _bacc.Bacc("TRN2", target_bir_lowering=False, num_devices=1)
    arrays, args = {}, {}
    for name, v in a.items():
        v = np.ascontiguousarray(v)
        arrays[f"in_{name}"] = v
        args[name] = nc.dram_tensor(f"in_{name}", v.shape, mybir.dt.from_np(v.dtype), kind="ExternalInput").ap()
    out_t = nc.dram_tensor("out_t", (P, KD, TOK), F32, kind="ExternalOutput").ap()
    build(nc, out_t=out_t, **args)
    r = _run(nc, [arrays], core_ids=[0])
    got = r.results[0]["out_t"]
    return np.ascontiguousarray(got.transpose(1, 0, 2).reshape(D, TOK).T.reshape(B, T, D))
```

```python
from contextlib import ExitStack

import numpy as np

import concourse.bass as bass
from concourse import mybir

F32 = mybir.dt.float32
F32R = mybir.dt.float32r
BF16 = mybir.dt.bfloat16
I32 = mybir.dt.int32
U32 = mybir.dt.uint32
ALU = mybir.AluOpType
ACT = mybir.ActivationFunctionType
AX = mybir.AxisListType

P = 128
B, T, D = 16, 256, 256
KD = D // P
NT = T // P
TOK = B * T
L, A = 10, 64
NH, HD = 16, 16
NP = NH // 2
SLOT = 64
MAX_ROW = 3 * HD
HID = 1024
KH = HID // P
E, PART = 16, 64
SHARED = D - PART
EPS = 1e-5
QSCALE = HD ** -0.5
HEAD = 1
HEAD_STARTED = "xa_split expert_split y_ready yc_split out_ready unit_mm prod_ready act_ready y_stored x1_stored x1_out c_act out_stored".split()

TW = 512
TILES = TOK // TW
BT = TW // T

W1_AT = 0
W2_AT = W1_AT + KD * HID
H1_AT = W2_AT + KD * HID
H2_AT = H1_AT + KH * HID
W3_AT = H2_AT + KH * HID
FFN_COLS = W3_AT + KH * D
LATE = (2, 5)
C_UNITS = 4 * KH + KD
FILLS = 6
UNITS = 2 * FILLS
SHARE = FFN_COLS // B
CHECK = FFN_COLS // TILES


def max_fill(f):
    return (0, 4 * f, 4) if f < 2 else (1, 2 * (f - 2), 2)


def score_fill(f):
    if f in LATE:
        return 4 * LATE.index(f), 4, P, P
    return 2 * [0, 1, None, 2, 3][f], 2, 0, 0


def build(nc, x_t, x_tok, lang, expert, cond_w1, cond_w2, cond_vec, w_qv, w_k, w_f, b_f, ident_d, mask_d, key_row_d,
          fc1_w, fc1_b, fc2_w, fc2_b, exp_w, exp_b, ffn_d, ffn_s, out_t):
    ctx = ExitStack()
    with ctx:
        def sb(name, shape, dt=F32, where=ctx):
            return where.enter_context(nc.sbuf_tensor(name, shape, dt))

        def sem(name):
            return ctx.enter_context(nc.semaphore(name))

        banks = [ctx.enter_context(nc.psum_tensor(f"bank{i}", [P, 512], F32)) for i in range(8)]
        ring, side, max_bank, score_bank = banks[0:2], banks[2:4], banks[4:6], banks[6:8]

        ffn_scratch = nc.dram_tensor("ffn_scratch", (P, FFN_COLS), F32).ap()
        x1_scratch = nc.dram_tensor("x1_scratch", (P, KD, TOK), F32).ap()
        y_scratch = nc.dram_tensor("y_scratch", (P, KD, TOK), F32).ap()

        ffn_w = sb("ffn_w", [P, FFN_COLS], F32R)
        fc1_bias = sb("fc1_bias", [P, KH])
        fc2_bias = sb("fc2_bias", [P, 1 + BT])
        scales = sb("scales", [P, 4 * KH + KD])
        low_bits = sb("low_bits", [P, 1])
        low_count = sb("low_count", [1, 1], I32)
        ones = sb("ones", [P, 1])
        xa = yc = sb("tile_in", [P, KD, TW])
        xa_hi = yc_hi = sb("tile_hi", [P, KD, TW], F32R)
        xa_lo = yc_lo = sb("tile_lo", [P, KD, TW], F32R)
        SC_W1, SC_W2, SC_H1, SC_H2 = (scales[:, i * KH:(i + 1) * KH] for i in range(4))
        SC_W3 = scales[:, 4 * KH:4 * KH + KD]

        s = {}
        for name in """
                sp_settled pool_settled dve_settled raw_loaded const_loaded ffn_copied ffn_loaded const_made ident_made row_made
                front_loaded hidden_mm hidden_out adapted_mm u_out norm_t_mm norm_t_out keys_mm keys_out qv_mm qv_out
                stats_ready moments_ready veps_ready rstd_ready norm_ready
                keys_hi keys_low q_hi q_low q_again keys_moved values_moved
                q_t_mm q_t_out max_mm max_out m2_hi m2_ready max_t_mm max_t_out maxima_moved
                score_mm exp_done masked early_mm early_out late_mm late_out
                pv_t_mm recip_done att_out att_t_mm att_t_out proj_mm x1_out resid_loaded x1_stored
                phase1_over phase2_over fc1_hi_made fc1_split fc2_loaded fc2_hi_made fc2_split
                xa_loaded xa_hi xa_split expert_loaded expert_hi expert_split bias_loaded
                unit_mm raw_ready hi_ready act_ready y_ready y_stored
                bits_step bits_max bits_summed flag_ready
                yc_loaded yc_hi yc_split resid2_loaded sil_ready prod_ready c_mm c_act c_hi c_ready
                out_ready out_stored""".split():
            s[name] = sem(name)

        early = ExitStack()
        fc1_hi = sb("fc1_hi", [P, KD, HID], F32R, early)
        fc1_lo = sb("fc1_lo", [P, KD, HID], F32R, early)

        one = ExitStack()
        xt = sb("xt", [P, KD, T], F32, one)
        xtok = sb("xtok", [P, NT, D], F32, one)
        w1c = sb("w1c", [P, KD, A], F32, one)
        w2c = sb("w2c", [A + 1, D], F32, one)
        vec = sb("vec", [P, 5], F32, one)
        wqv = sb("wqv", [P, KD, D + HD], F32, one)
        wk = sb("wk", [P, KD, P], F32, one)
        wf = sb("wf", [P, KD, D], F32, one)
        bf = sb("bf", [P, KD], F32, one)
        ident = sb("ident", [P, P], F32, one)
        ident_b = sb("ident_b", [P, P], BF16, one)
        mask = sb("mask", [P, 4, P], BF16, one)
        key_row = sb("key_row", [P, 1], F32, one)
        h_t = sb("h_t", [A + 1, T], F32, one)
        u = sb("u", [P, NT, D], F32, one)
        stats = sb("stats", [P, NT, 6], F32, one)
        moments = sb("moments", [P, NT, 2], F32, one)
        veps = sb("veps", [P, NT], F32, one)
        half = sb("half", [P, NT], F32, one)
        rstd = sb("rstd", [P, NT], F32, one)
        norm = sb("norm", [P, NT, D], F32, one)
        norm_t = sb("norm_t", [P, KD, T], F32, one)
        q_parts = sb("q_parts", [P, NT, NH, SLOT], F32, one)
        q_t = [sb(f"q_t{i}", [P, NP, T], F32R, one) for i in range(2)]
        keys = [sb(f"keys{i}", [P, T], F32R, one) for i in range(2)]
        values = [sb(f"values{i}", [P, NT, 32], F32, one) for i in range(2)]
        keys_new = sb("keys_new", [P, T], F32R, one)
        values_new = sb("values_new", [P, NT, 32], F32, one)
        pv = sb("pv", [P, 4, T], F32, one)
        neg_max = sb("neg_max", [P, NT, NP, 2], F32, one)
        m2 = sb("m2", [P, NT, 2, 2, NP], F32, one)
        m_t = sb("m_t", [4 * NP, T], F32R, one)
        p0 = sb("p0", [P, 4, 2, 2, T], F32, one)
        p1 = sb("p1", [P, 2, 2, 4, P], F32, one)
        fc1_raw = sb("fc1_raw", [P, HID], F32, one)
        recip = sb("recip", [P, NT, NH], F32, one)
        att = sb("att", [P, NT, D], F32, one)
        att_t = sb("att_t", [P, KD, T], F32, one)
        resid = sb("resid", [P, KD, T], F32, one)
        x1 = sb("x1", [P, KD, T], F32, one)
        one.close()

        two = ExitStack()
        fc2_raw = sb("fc2_raw", [P, KH, SHARED], F32, two)
        fc2a_hi = sb("fc2a_hi", [P, KH, P], F32R, two)
        fc2a_lo = sb("fc2a_lo", [P, KH, P], F32R, two)
        fc2b_hi = sb("fc2b_hi", [P, KH, BT, P], F32R, two)
        fc2b_lo = sb("fc2b_lo", [P, KH, BT, P], F32R, two)
        exp_raw = sb("exp_raw", [P, BT, KH, PART], F32, two)
        g_hi = sb("g_hi", [P, KH, TW], F32R, two)
        g_lo = sb("g_lo", [P, KH, TW], F32R, two)
        g_raw = sb("g_raw", [P, 2, TW], F32, two)
        y = sb("y", [P, KD, TW], F32, two)
        bits = sb("bits", [P, CHECK], U32, two)
        bits_top = sb("bits_top", [P, 1], U32, two)
        two.close()
        early.close()

        three = ExitStack()
        h_hi = [sb(f"h{i}_hi", [P, KH, TW], F32R, three) for i in range(2)]
        h_lo = [sb(f"h{i}_lo", [P, KH, TW], F32R, three) for i in range(2)]
        sil = sb("sil", [P, 2, TW], F32, three)
        h_raw = sb("h_raw", [P, 2, TW], F32, three)
        resid2 = sb("resid2", [P, KD, TW], F32, three)
        outs = sb("outs", [P, KD, TW], F32, three)
        three.close()

        block = ctx.enter_context(nc.Block())

        def is_first(n):
            return isinstance(n, int) and n == 0

        def all_iterations(eng, iteration):
            iteration(-1, 1, True, True, False, False)
            iteration(0, 0, True, True, True, False)
            with eng.Fori(0, (B - 4) // 2) as pair:
                for step in (1, 2):
                    iteration(2 * pair + step, step % 2, True, True, True, True)
            iteration(B - 3, 1, True, True, True, True)
            iteration(B - 2, 0, False, True, True, True)
            iteration(B - 1, 1, False, False, True, True)

        def settle(eng, name):
            eng.sem_inc(s[name], 1)

        @block.sync
        def _(sp):
            def load_front(n):
                l = sp.value_load(lang[0:1, bass.ds(n, 1)], min_val=0, max_val=L - 1)
                if not is_first(n):
                    sp.wait_ge(s["adapted_mm"], n)
                sp.dma_start(xt[:, :, :], x_t[:, :, bass.ds(n * T, T)]).then_inc(s["front_loaded"], 16)
                sp.dma_start(w1c[:, :, :], cond_w1[bass.ds(l, 1)].rearrange("a p k h -> p (a k) h")).then_inc(s["front_loaded"], 16)
                sp.dma_start(w2c[:, :], cond_w2[bass.ds(l, 1)].rearrange("a p h -> p (a h)")).then_inc(s["front_loaded"], 16)
                if not is_first(n):
                    sp.wait_ge(s["u_out"], n)
                    sp.wait_ge(s["norm_t_out"], n)
                    settle(sp, "sp_settled")
                sp.dma_start(xtok[:, :, :], x_tok[bass.ds(n, 1)].rearrange("a p t d -> p (a t) d")).then_inc(s["front_loaded"], 16)
                sp.dma_start(vec[:, :], cond_vec[bass.ds(l, 1)].rearrange("a p c -> p (a c)")).then_inc(s["front_loaded"], 16)

            def load_resid(b):
                if not is_first(b):
                    sp.wait_ge(s["x1_out"], HEAD + KD * b)
                sp.dma_start(resid[:, :, :], x_t[:, :, bass.ds(b * T, T)]).then_inc(s["resid_loaded"], 16)

            def move_maxima(n, odd):
                sp.wait_ge(s["max_t_out"], n + 1)
                settle(sp, "sp_settled")
                for par in range(2):
                    for part in range(2):
                        row, at = SLOT * par + MAX_ROW + part, (2 * par + part) * NP
                        sp.dma_start(q_t[odd][row:row + 1, :, :].bitcast(F32), m_t[at:at + NP, :].bitcast(F32)).then_inc(s["maxima_moved"], 16)

            def store_x1(b):
                sp.wait_ge(s["x1_out"], HEAD + KD * (b + 1))
                sp.dma_start(x1_scratch[:, :, bass.ds(b * T, T)], x1[:, :, :]).then_inc(s["x1_stored"], 16)

            def store_ffn(b):
                cols = bass.ds(b * SHARE, SHARE)
                sp.dma_start(ffn_scratch[:, cols], ffn_d[:, cols]).then_inc(s["ffn_copied"], 16)

            def load_ffn(b):
                cols = bass.ds(b * SHARE, SHARE)
                sp.wait_ge(s["ffn_copied"], 16 * (b + 1))
                settle(sp, "sp_settled")
                sp.dma_start(ffn_w[:, cols].bitcast(F32), ffn_scratch[:, cols]).then_inc(s["ffn_loaded"], 16)

            load_front(0)
            sp.dma_start(ident[:, :], ident_d).then_inc(s["const_loaded"], 16)
            sp.dma_start(wqv[:, :, :], w_qv).then_inc(s["const_loaded"], 16)
            sp.dma_start(wk[:, :, :], w_k).then_inc(s["const_loaded"], 16)
            sp.dma_start(wf[:, :, :], w_f).then_inc(s["const_loaded"], 16)
            sp.dma_start(bf[:, :], b_f).then_inc(s["const_loaded"], 16)
            sp.dma_start(mask[:, :, :], mask_d).then_inc(s["const_loaded"], 16)
            sp.dma_start(key_row[:, :], key_row_d).then_inc(s["const_loaded"], 16)
            load_resid(0)
            sp.dma_start(fc1_raw[:, :], fc1_w[:, 0]).then_inc(s["raw_loaded"], 16)
            sp.dma_start(fc1_bias[:, :], fc1_b).then_inc(s["raw_loaded"], 16)
            sp.dma_start(scales[:, :], ffn_s).then_inc(s["raw_loaded"], 16)
            load_front(1)
            load_front(2)
            store_ffn(0)
            load_ffn(0)
            move_maxima(0, 0)
            load_front(3)
            store_ffn(1)
            load_ffn(1)
            move_maxima(1, 1)
            with sp.Fori(0, (B - 4) // 2) as pair:
                for step in (1, 2):
                    b = 2 * pair + step
                    store_ffn(b + 1)
                    load_front(b + 3)
                    load_ffn(b + 1)
                    store_x1(b - 1)
                    load_resid(b)
                    move_maxima(b + 1, 1 - step % 2)
            sp.wait_ge(s["x1_stored"], HEAD + 16 * BT)
            sp.dma_start(xa[:, :, :], x1_scratch[:, :, 0:TW]).then_inc(s["xa_loaded"], 16)
            for b in range(B - 3, B + 1):
                if b < B - 1:
                    store_ffn(b + 1)
                    load_ffn(b + 1)
                store_x1(b - 1)
                if b < B:
                    load_resid(b)
                if b < B - 1:
                    move_maxima(b + 1, (b + 1) % 2)
                if b == B - 2:
                    sp.wait_ge(s["fc1_split"], 1)
                    sp.dma_start(fc1_raw[:, :], fc1_w[:, 1]).then_inc(s["raw_loaded"], 16)
            sp.wait_ge(s["x1_stored"], HEAD + 16 * B)
            sp.wait_ge(s["phase1_over"], 4)

            sp.dma_start(fc2_raw[:, :, :], fc2_w).then_inc(s["fc2_loaded"], 16)

            def load_expert(t):
                for j in range(BT):
                    e = sp.value_load(expert[0:1, bass.ds(t * BT + j, 1)], min_val=0, max_val=E - 1)
                    sp.dma_start(exp_raw[:, j], exp_w[bass.ds(e, 1)].rearrange("a p k h -> p (a k) h")).then_inc(s["expert_loaded"], 16)
                    sp.dma_start(fc2_bias[SHARED - P:P, 1 + j:2 + j], exp_b[bass.ds(e, 1)].rearrange("a p o -> p (a o)")).then_inc(s["bias_loaded"], 16)

            sp.dma_start(fc2_bias[:, 0:1], fc2_b[0]).then_inc(s["bias_loaded"], 16)
            for j in range(BT):
                sp.dma_start(fc2_bias[0:SHARED - P, 1 + j:2 + j], fc2_b[1, 0:SHARED - P]).then_inc(s["bias_loaded"], 16)

            def load_x(t):
                sp.wait_ge(s["xa_split"], HEAD + t)
                sp.dma_start(xa[:, :, :], x1_scratch[:, :, bass.ds(t * TW, TW)]).then_inc(s["xa_loaded"], 16)

            def cond2_tile(t, more):
                if not is_first(t):
                    sp.wait_ge(s["expert_split"], HEAD + BT * t)
                    sp.wait_ge(s["y_ready"], HEAD + (1 + BT) * t)
                    settle(sp, "sp_settled")
                load_expert(t)
                if more:
                    load_x(t + 1)
                else:
                    sp.wait_ge(s["xa_split"], HEAD + TILES)
                    sp.wait_ge(s["y_stored"], HEAD + 16)
                    sp.dma_start(yc[:, :, :], y_scratch[:, :, 0:TW]).then_inc(s["yc_loaded"], 16)
                sp.wait_ge(s["y_ready"], HEAD + (1 + BT) * (t + 1))
                sp.dma_start(y_scratch[:, :, bass.ds(t * TW, TW)], y[:, :, :]).then_inc(s["y_stored"], 16)

            with sp.Fori(0, TILES - 1) as t:
                cond2_tile(t, True)
            cond2_tile(TILES - 1, False)
            sp.wait_ge(s["y_stored"], HEAD + 16 * TILES)
            sp.wait_ge(s["phase2_over"], 4)

            def load_y(t):
                sp.wait_ge(s["yc_split"], HEAD + t)
                sp.dma_start(yc[:, :, :], y_scratch[:, :, bass.ds(t * TW, TW)]).then_inc(s["yc_loaded"], 16)

            def ffn_tile(t, more):
                if not is_first(t):
                    sp.wait_ge(s["out_ready"], HEAD + KD * t)
                sp.dma_start(resid2[:, :, :], x1_scratch[:, :, bass.ds(t * TW, TW)]).then_inc(s["resid2_loaded"], 16)
                if more:
                    load_y(t + 1)
                sp.wait_ge(s["out_ready"], HEAD + KD * (t + 1))
                sp.dma_start(out_t[:, :, bass.ds(t * TW, TW)], outs[:, :, :]).then_inc(s["out_stored"], 16)

            with sp.Fori(0, TILES - 1) as t:
                ffn_tile(t, True)
            ffn_tile(TILES - 1, False)
            sp.wait_ge(s["out_stored"], HEAD + 16 * TILES)

        @block.gpsimd
        def _(pool):
            for name in HEAD_STARTED:
                pool.sem_inc(s[name], HEAD)
            nc.gpsimd.memset(q_parts[:, :, :, :], 0.0).then_inc(s["const_made"], 1)
            nc.gpsimd.memset(half[:, :], -0.5).then_inc(s["const_made"], 1)
            nc.gpsimd.memset(values_new[:, :, :], 0.0).then_inc(s["const_made"], 1)
            pool.wait_ge(s["const_made"], 3)
            nc.gpsimd.memset(values_new[:, :, HD:HD + 1], 1.0).then_inc(s["const_made"], 1)
            nc.gpsimd.memset(ones[:, :], 1.0).then_inc(s["const_made"], 1)
            pool.wait_ge(s["const_loaded"], 112)
            nc.gpsimd.tensor_copy(ident_b[:, :], ident[:, :]).then_inc(s["ident_made"], 1)

            def rstd_of(n):
                pool.wait_ge(s["veps_ready"], n + 1)
                if isinstance(n, int) and n == 0:
                    pool.wait_ge(s["const_made"], 5)
                nc.gpsimd.tensor_tensor(rstd[:, :], veps[:, :], half[:, :], ALU.pow).then_inc(s["rstd_ready"], 1)

            def high_again(n, t):
                pool.wait_ge(s["q_hi"], NT * n + t + 1)
                settle(pool, "pool_settled")
                nc.gpsimd.tensor_copy(q_parts[:, t, :, 2 * HD:3 * HD], q_parts[:, t, :, 0:HD]).then_inc(s["q_again"], 1)

            def move_keys(n, odd, late):
                pool.wait_ge(s["keys_low"], n + 1)
                pool.wait_ge(s["keys_out"], n + 1)
                if late:
                    pool.wait_ge(s["score_mm"], UNITS * (n - 1))
                settle(pool, "pool_settled")
                nc.gpsimd.tensor_copy(keys[odd][:, :], keys_new[:, :].bitcast(F32)).then_inc(s["keys_moved"], 1)

            def move_values(n, odd, late):
                pool.wait_ge(s["qv_out"], NT * (n + 1))
                if late:
                    pool.wait_ge(s["late_mm"], n - 1)
                settle(pool, "pool_settled")
                nc.gpsimd.tensor_copy(values[odd][:, :, :], values_new[:, :, :]).then_inc(s["values_moved"], 1)

            def causal(b, f):
                pool.wait_ge(s["exp_done"], UNITS * b + 2 * f + 2)
                settle(pool, "pool_settled")
                first = score_fill(f)[0]
                v = p1[:, first // 4] if f in LATE else p0[:, first // 2]
                v = v.rearrange("p a c t -> p (a c) t")[:, :, 0:P]
                nc.gpsimd.affine_select(out=v, in_=v, compare_op=ALU.is_ge, fill=0.0, base=0,
                                        pattern=[[0, v.shape[1]], [1, P]], channel_multiplier=-1).then_inc(s["masked"], 1)

            def iteration(b, odd, front, maxima, softmax, tail):
                if maxima:
                    move_values(b + 1, 1 - odd, tail)
                if softmax:
                    causal(b, 0)
                if front:
                    rstd_of(b + 2)
                if softmax:
                    for f in range(1, 4):
                        causal(b, f)
                if front:
                    high_again(b + 2, 0)
                if softmax:
                    causal(b, 4)
                if front:
                    move_keys(b + 2, odd, softmax)
                if softmax:
                    causal(b, 5)
                if front:
                    high_again(b + 2, 1)

            rstd_of(0)
            move_keys(0, 0, False)
            high_again(0, 0)
            high_again(0, 1)
            all_iterations(pool, iteration)
            pool.wait_ge(s["masked"], FILLS * B)
            pool.sem_inc(s["phase1_over"], 1)
            pool.wait_ge(s["phase1_over"], 4)

            pool.wait_ge(s["x1_stored"], HEAD + 16 * B)
            nc.gpsimd.memset(bits[:, :], 0.0).then_inc(s["bits_step"], 1)
            with pool.Fori(0, TILES) as t:
                pool.wait_ge(s["expert_loaded"], 16 * BT * (t + 1))
                pool.wait_ge(s["unit_mm"], HEAD + (KH + KD) * t)
                settle(pool, "pool_settled")
                for j in range(BT):
                    nc.gpsimd.tensor_copy(fc2b_hi[:, :, j, SHARED - P:P], exp_raw[:, j]).then_inc(s["expert_hi"], 1)
                pool.wait_ge(s["expert_hi"], BT * (t + 1))
                for j in range(BT):
                    nc.gpsimd.tensor_tensor(fc2b_lo[:, :, j, SHARED - P:P], exp_raw[:, j], fc2b_hi[:, :, j, SHARED - P:P].bitcast(F32), ALU.subtract).then_inc(s["expert_split"], 1)
            pool.wait_ge(s["expert_split"], HEAD + BT * TILES)
            pool.sem_inc(s["phase2_over"], 1)

        @block.scalar
        def _(act):
            def hidden(n):
                act.wait_ge(s["hidden_mm"], n + 1)
                nc.scalar.activation(h_t[0:A, :], side[0][0:A, 0:T], ACT.Relu, bias=vec[0:A, 4:5]).then_inc(s["hidden_out"], 1)

            def affine(n):
                act.wait_ge(s["norm_t_mm"], n + 1)
                for k in range(KD):
                    last = nc.scalar.activation(norm_t[:, k, :], side[0][:, k * T:(k + 1) * T], ACT.Identity,
                                                bias=vec[:, 2 + k:3 + k], scale=vec[:, k:k + 1])
                last.then_inc(s["norm_t_out"], 1)

            def queries_out(n, odd, t, j):
                act.wait_ge(s["q_t_mm"], 4 * n + 2 * t + j + 1)
                nc.scalar.activation(q_t[odd][:, 4 * j:4 * (j + 1), t * P:(t + 1) * P], ring[j][:, :].rearrange("p (c t) -> p c t", c=4),
                                     ACT.Copy).then_inc(s["q_t_out"], 1)

            def exponential(b, u):
                act.wait_ge(s["score_mm"], UNITS * b + u + 1)
                f, par = u // 2, u % 2
                first = score_fill(f)[0]
                dst = p1[:, first // 4, par] if f in LATE else p0[:, first // 2, par]
                nc.scalar.activation(dst.rearrange("p c t -> p (c t)"), score_bank[par][:, :], ACT.Exp).then_inc(s["exp_done"], 1)

            def products_out(b, late):
                act.wait_ge(s["late_mm" if late else "early_mm"], b + 1)
                g = 2 if late else 0
                nc.scalar.activation(pv[:, g:g + 2, :], ring[0 if late else 1][:, :].rearrange("p (g t) -> p g t", g=2),
                                     ACT.Copy).then_inc(s["late_out" if late else "early_out"], 1)

            def attention_out(b):
                act.wait_ge(s["att_t_mm"], b + 1)
                nc.scalar.activation(att_t[:, :, :], side[1][:, :].rearrange("p (k t) -> p k t", k=KD), ACT.Copy).then_inc(s["att_t_out"], 1)

            def maxima_out(n):
                act.wait_ge(s["max_t_mm"], n + 1)
                if not is_first(n):
                    act.wait_ge(s["maxima_moved"], 64 * n)
                nc.scalar.activation(m_t[:, :], max_bank[1][0:4 * NP, 0:T], ACT.Copy).then_inc(s["max_t_out"], 1)

            def iteration(b, odd, front, maxima, softmax, tail):
                if maxima:
                    queries_out(b + 1, 1 - odd, 0, 0)
                    queries_out(b + 1, 1 - odd, 0, 1)
                if front:
                    hidden(b + 2)
                if tail:
                    products_out(b - 1, True)
                if softmax:
                    for u in range(0, 4):
                        exponential(b, u)
                if maxima:
                    queries_out(b + 1, 1 - odd, 1, 0)
                    queries_out(b + 1, 1 - odd, 1, 1)
                if softmax:
                    for u in range(4, 8):
                        exponential(b, u)
                    products_out(b, False)
                if front:
                    affine(b + 2)
                if tail:
                    attention_out(b - 1)
                if softmax:
                    for u in range(8, 12):
                        exponential(b, u)
                if maxima:
                    maxima_out(b + 1)

            act.wait_ge(s["front_loaded"], 80)
            hidden(0)
            affine(0)
            all_iterations(act, iteration)
            products_out(B - 1, True)
            attention_out(B - 1)
            act.wait_ge(s["att_t_out"], B)
            act.sem_inc(s["phase1_over"], 1)
            act.wait_ge(s["phase1_over"], 4)

            with act.Fori(0, TILES) as t:
                for m in range(KH):
                    act.wait_ge(s["unit_mm"], HEAD + (KH + KD) * t + m + 1)
                    if m >= 2:
                        act.wait_ge(s["act_ready"], HEAD + KH * t + m - 1)
                    else:
                        act.wait_ge(s["act_ready"], HEAD + KH * t)
                    nc.scalar.activation(g_raw[:, m % 2, :], banks[m % 6][:, :], ACT.Gelu, bias=fc1_bias[:, m:m + 1]).then_inc(s["raw_ready"], 1)
            act.wait_ge(s["raw_ready"], KH * TILES)
            act.sem_inc(s["phase2_over"], 1)
            act.wait_ge(s["phase2_over"], 4)

            with act.Fori(0, TILES) as t:
                for m in range(KH):
                    act.wait_ge(s["c_mm"], C_UNITS * t + 2 * m + 1)
                    if m >= 2:
                        act.wait_ge(s["prod_ready"], HEAD + KH * t + m - 1)
                    else:
                        act.wait_ge(s["prod_ready"], HEAD + KH * t)
                    nc.scalar.activation(sil[:, m % 2, :], banks[(2 * m) % 8][:, :], ACT.Silu, scale=SC_W1[:, m:m + 1]).then_inc(s["sil_ready"], 1)
                for layer in range(2):
                    for m in range(KH):
                        g = 2 * KH + layer * KH + m
                        act.wait_ge(s["c_mm"], C_UNITS * t + g + 1)
                        act.wait_ge(s["c_ready"], 3 * KH * t + (1 + layer) * KH + m - 1)
                        sc = (SC_H1, SC_H2)[layer]
                        nc.scalar.activation(h_raw[:, m % 2, :], banks[g % 8][:, :], ACT.Gelu, scale=sc[:, m:m + 1]).then_inc(s["c_act"], 1)

        @block.vector
        def _(dve):
            def add_adapted(n):
                dve.wait_ge(s["adapted_mm"], n + 1)
                nc.vector.tensor_tensor(u[:, :, :], side[1][:, :].rearrange("p (t d) -> p t d", t=NT), xtok[:, :, :], ALU.add).then_inc(s["u_out"], 1)
                dve.wait_ge(s["u_out"], n + 1)
                for t in range(NT):
                    nc.vector.bn_stats(stats[:, t, :], u[:, t, :]).then_inc(s["stats_ready"], 1)
                dve.wait_ge(s["stats_ready"], NT * (n + 1))
                settle(dve, "dve_settled")
                for t in range(NT):
                    nc.vector.bn_aggr(moments[:, t, :], stats[:, t, :]).then_inc(s["moments_ready"], 1)
                dve.wait_ge(s["moments_ready"], NT * (n + 1))
                nc.vector.tensor_scalar(veps[:, :], moments[:, :, 1], EPS, None, ALU.add).then_inc(s["veps_ready"], 1)

            def normalise(n):
                dve.wait_ge(s["rstd_ready"], n + 1)
                for t in range(NT):
                    nc.vector.tensor_scalar(norm[:, t, :], u[:, t, :], moments[:, t, 0:1], rstd[:, t:t + 1],
                                            ALU.subtract, ALU.mult).then_inc(s["norm_ready"], 1)

            def keys_of(n):
                dve.wait_ge(s["keys_mm"], n + 1)
                if not is_first(n):
                    dve.wait_ge(s["keys_moved"], n)
                src = side[0]
                nc.vector.tensor_scalar(keys_new[:, :], src[:, 0:T], key_row[:, :], None, ALU.add).then_inc(s["keys_hi"], 1)
                dve.wait_ge(s["keys_hi"], n + 1)
                nc.vector.tensor_tensor(keys_new[32:64, :], src[32:64, 0:T], keys_new[32:64, :].bitcast(F32), ALU.subtract).then_inc(s["keys_low"], 1)
                nc.vector.tensor_tensor(keys_new[96:128, :], src[96:128, 0:T], keys_new[96:128, :].bitcast(F32), ALU.subtract).then_inc(s["keys_out"], 1)

            def queries_of(n, t):
                dve.wait_ge(s["qv_mm"], NT * n + t + 1)
                if not is_first(n):
                    dve.wait_ge(s["values_moved"], n)
                src = max_bank[0] if t else side[1]
                q = src[:, 0:D].rearrange("p (h c) -> p h c", h=NH)
                nc.vector.tensor_scalar(q_parts[:, t, :, 0:HD].bitcast(F32R), q, QSCALE, None, ALU.mult).then_inc(s["q_hi"], 1)
                dve.wait_ge(s["q_hi"], NT * n + t + 1)
                nc.vector.scalar_tensor_tensor(out=q_parts[:, t, :, HD:2 * HD].bitcast(F32R), in0=q, scalar=QSCALE, in1=q_parts[:, t, :, 0:HD],
                                               op0=ALU.mult, op1=ALU.subtract).then_inc(s["q_low"], 1)
                nc.vector.tensor_copy(values_new[:, t, 0:HD], src[:, D:D + HD]).then_inc(s["qv_out"], 1)

            def maximum(n, u):
                dve.wait_ge(s["max_mm"], UNITS * n + u + 1)
                t, first, pairs = max_fill(u // 2)
                nc.vector.tensor_reduce(neg_max[:, t, first:first + pairs, u % 2],
                                        max_bank[u % 2][:, :].rearrange("p (c k) -> p c k", c=pairs),
                                        AX.X, ALU.max, negate=True).then_inc(s["max_out"], 1)

            def split_fc1(k):
                dve.wait_ge(s["raw_loaded"], 48 + 16 * k)
                nc.vector.tensor_copy(fc1_hi[:, k, :], fc1_raw[:, :]).then_inc(s["fc1_hi_made"], 1)
                dve.wait_ge(s["fc1_hi_made"], k + 1)
                nc.vector.tensor_tensor(fc1_lo[:, k, :], fc1_raw[:, :], fc1_hi[:, k, :].bitcast(F32), ALU.subtract).then_inc(s["fc1_split"], 1)

            def split_maxima(b):
                dve.wait_ge(s["max_out"], UNITS * (b + 1))
                nm = neg_max[:, :, :, :].rearrange("p t c a -> p t a c")
                nc.vector.tensor_copy(m2[:, :, :, 0, :].bitcast(F32R), nm).then_inc(s["m2_hi"], 1)
                dve.wait_ge(s["m2_hi"], b + 1)
                nc.vector.tensor_tensor(m2[:, :, :, 1, :].bitcast(F32R), nm, m2[:, :, :, 0, :], ALU.subtract).then_inc(s["m2_ready"], 1)

            def attention(b, t):
                dve.wait_ge(s["pv_t_mm"], NT * b + t + 1)
                o = side[t][:, :].rearrange("p (h c) -> p h c", h=NH)
                nc.vector.reciprocal(recip[:, t, :], o[:, :, HD]).then_inc(s["recip_done"], 1)
                dve.wait_ge(s["recip_done"], NT * b + t + 1)
                nc.vector.tensor_tensor(att[:, t, :].rearrange("p (h c) -> p h c", h=NH), o[:, :, 0:HD],
                                        recip[:, t, :].rearrange("p (h c) -> p h c", c=1).broadcast_to([P, NH, HD]), ALU.mult).then_inc(s["att_out"], 1)

            def add_residual(b):
                dve.wait_ge(s["resid_loaded"], 16 * (b + 1))
                dve.wait_ge(s["x1_stored"], HEAD + 16 * b)
                dve.wait_ge(s["proj_mm"], b + 1)
                for m in range(KD):
                    nc.vector.scalar_tensor_tensor(out=x1[:, m, :], in0=side[0][:, m * T:(m + 1) * T], scalar=bf[:, m:m + 1], in1=resid[:, m, :],
                                                   op0=ALU.add, op1=ALU.add).then_inc(s["x1_out"], 1)

            def iteration(b, odd, front, maxima, softmax, tail):
                if not maxima:
                    split_fc1(0)
                if maxima:
                    maximum(b + 1, 0)
                    maximum(b + 1, 1)
                if front:
                    add_adapted(b + 2)
                if maxima:
                    maximum(b + 1, 2)
                    maximum(b + 1, 3)
                if tail:
                    attention(b - 1, 0)
                if maxima:
                    maximum(b + 1, 4)
                if tail:
                    attention(b - 1, 1)
                if maxima:
                    maximum(b + 1, 5)
                if front:
                    normalise(b + 2)
                if maxima:
                    for u in range(6, 10):
                        maximum(b + 1, u)
                if front:
                    keys_of(b + 2)
                if maxima:
                    maximum(b + 1, 10)
                    maximum(b + 1, 11)
                    split_maxima(b + 1)
                if front:
                    queries_of(b + 2, 0)
                if tail:
                    add_residual(b - 1)
                if front:
                    queries_of(b + 2, 1)

            def split_x(t):
                dve.wait_ge(s["xa_loaded"], 16 * (t + 1))
                if not is_first(t):
                    dve.wait_ge(s["unit_mm"], HEAD + (KH + KD) * (t - 1) + KH)
                nc.vector.tensor_copy(xa_hi[:, :, :], xa[:, :, :]).then_inc(s["xa_hi"], 1)
                dve.wait_ge(s["xa_hi"], t + 1)
                nc.vector.tensor_tensor(xa_lo[:, :, :], xa[:, :, :], xa_hi[:, :, :].bitcast(F32), ALU.subtract).then_inc(s["xa_split"], 1)

            nc.vector.memset(h_t[A:A + 1, :], 1.0).then_inc(s["row_made"], 1)
            dve.wait_ge(s["front_loaded"], 80)
            add_adapted(0)
            normalise(0)
            dve.wait_ge(s["const_made"], 5)
            dve.wait_ge(s["const_loaded"], 112)
            keys_of(0)
            queries_of(0, 0)
            queries_of(0, 1)
            all_iterations(dve, iteration)
            split_fc1(1)
            split_x(0)
            attention(B - 1, 0)
            attention(B - 1, 1)
            add_residual(B - 1)
            dve.wait_ge(s["x1_out"], HEAD + KD * B)
            dve.wait_ge(s["fc1_split"], KD)
            dve.sem_inc(s["phase1_over"], 1)
            dve.wait_ge(s["phase1_over"], 4)

            dve.wait_ge(s["ffn_loaded"], 16 * B)
            def split_y(t):
                dve.wait_ge(s["yc_loaded"], 16 * (t + 1))
                if is_first(t):
                    dve.wait_ge(s["unit_mm"], HEAD + (KH + KD) * (TILES - 1) + KH)
                else:
                    dve.wait_ge(s["c_mm"], C_UNITS * (t - 1) + 2 * KH)
                nc.vector.tensor_copy(yc_hi[:, :, :], yc[:, :, :]).then_inc(s["yc_hi"], 1)
                dve.wait_ge(s["yc_hi"], t + 1)
                nc.vector.tensor_tensor(yc_lo[:, :, :], yc[:, :, :], yc_hi[:, :, :].bitcast(F32), ALU.subtract).then_inc(s["yc_split"], 1)

            def or_bits(t):
                dve.wait_ge(s["bits_step"], t + 1)
                nc.vector.tensor_tensor(bits[:, :], bits[:, :], ffn_w[:, bass.ds(t * CHECK, CHECK)].bitcast(U32), ALU.bitwise_or).then_inc(s["bits_step"], 1)

            def split_fc2b():
                for j in range(BT):
                    nc.vector.tensor_copy(fc2b_hi[:, :, j, 0:SHARED - P], fc2_raw[:, :, P:SHARED]).then_inc(s["fc2_hi_made"], 1)
                dve.wait_ge(s["fc2_hi_made"], 1 + BT)
                for j in range(BT):
                    nc.vector.tensor_tensor(fc2b_lo[:, :, j, 0:SHARED - P], fc2_raw[:, :, P:SHARED], fc2b_hi[:, :, j, 0:SHARED - P].bitcast(F32),
                                            ALU.subtract).then_inc(s["fc2_split"], 1)

            def cond2_tile(t, more):
                if not more:
                    or_bits(t)
                for m in range(KH):
                    dve.wait_ge(s["raw_ready"], KH * t + m + 1)
                    nc.vector.tensor_copy(g_hi[:, m, :], g_raw[:, m % 2, :]).then_inc(s["hi_ready"], 1)
                    dve.wait_ge(s["hi_ready"], KH * t + m + 1)
                    nc.vector.tensor_tensor(g_lo[:, m, :], g_raw[:, m % 2, :], g_hi[:, m, :].bitcast(F32), ALU.subtract).then_inc(s["act_ready"], 1)
                if more:
                    if is_first(t):
                        split_fc2b()
                    split_x(t + 1)
                    or_bits(t)
                else:
                    split_y(0)
                    dve.wait_ge(s["bits_step"], TILES + 1)
                    nc.vector.tensor_scalar(bits[:, :], bits[:, :], 0xFFF, None, ALU.bitwise_and).then_inc(s["bits_step"], 1)
                    dve.wait_ge(s["bits_step"], TILES + 2)
                    nc.vector.tensor_reduce(bits_top[:, :], bits[:, :], AX.X, ALU.max).then_inc(s["bits_step"], 1)
                    dve.wait_ge(s["bits_step"], TILES + 3)
                    nc.vector.tensor_copy(low_bits[:, :], bits_top[:, :]).then_inc(s["bits_max"], 1)
                dve.wait_ge(s["bias_loaded"], 16 * (1 + BT) + 16 * BT * (t + 1))
                if not is_first(t):
                    dve.wait_ge(s["y_stored"], HEAD + 16 * t)
                dve.wait_ge(s["unit_mm"], HEAD + (KH + KD) * t + KH + 1)
                nc.vector.tensor_scalar(y[:, 0, :], banks[6][:, :], fc2_bias[:, 0:1], None, ALU.add).then_inc(s["y_ready"], 1)
                dve.wait_ge(s["unit_mm"], HEAD + (KH + KD) * t + KH + 2)
                for j in range(BT):
                    nc.vector.tensor_scalar(y[:, 1, j * T:(j + 1) * T], banks[7][:, j * T:(j + 1) * T], fc2_bias[:, 1 + j:2 + j], None, ALU.add).then_inc(s["y_ready"], 1)

            def split_fc2a():
                dve.wait_ge(s["fc2_loaded"], 16)
                nc.vector.tensor_copy(fc2a_hi[:, :, :], fc2_raw[:, :, 0:P]).then_inc(s["fc2_hi_made"], 1)
                dve.wait_ge(s["fc2_hi_made"], 1)
                nc.vector.tensor_tensor(fc2a_lo[:, :, :], fc2_raw[:, :, 0:P], fc2a_hi[:, :, :].bitcast(F32), ALU.subtract).then_inc(s["fc2_split"], 1)

            split_fc2a()
            cond2_tile(0, True)
            with dve.Fori(1, TILES - 1) as t:
                cond2_tile(t, True)
            cond2_tile(TILES - 1, False)
            dve.wait_ge(s["bits_summed"], 1)
            nc.vector.tensor_copy(low_count[:, :], banks[2][0:1, 0:1]).then_inc(s["flag_ready"], 1)
            dve.wait_ge(s["y_ready"], HEAD + 3 * TILES)
            dve.wait_ge(s["flag_ready"], 1)
            dve.sem_inc(s["phase2_over"], 1)
            dve.wait_ge(s["phase2_over"], 4)

            def split(dst_hi, dst_lo, src, done):
                nc.vector.tensor_copy(dst_hi, src).then_inc(s["c_hi"], 1)
                dve.wait_ge(s["c_hi"], done + 1)
                nc.vector.tensor_tensor(dst_lo, src, dst_hi.bitcast(F32), ALU.subtract).then_inc(s["c_ready"], 1)

            def ffn_tile(t, more):
                for m in range(KH):
                    dve.wait_ge(s["sil_ready"], KH * t + m + 1)
                    dve.wait_ge(s["c_mm"], C_UNITS * t + 2 * m + 2)
                    if m < 2 and not is_first(t):
                        dve.wait_ge(s["c_ready"], 3 * KH * t)
                    nc.vector.scalar_tensor_tensor(out=h_raw[:, m % 2, :], in0=banks[(2 * m + 1) % 8][:, :], scalar=SC_W2[:, m:m + 1],
                                                   in1=sil[:, m % 2, :], op0=ALU.mult, op1=ALU.mult).then_inc(s["prod_ready"], 1)
                    dve.wait_ge(s["prod_ready"], HEAD + KH * t + m + 1)
                    split(h_hi[0][:, m, :], h_lo[0][:, m, :], h_raw[:, m % 2, :], 3 * KH * t + m)
                for layer in range(2):
                    for m in range(KH):
                        dve.wait_ge(s["c_act"], HEAD + 2 * KH * t + layer * KH + m + 1)
                        split(h_hi[1 - layer][:, m, :], h_lo[1 - layer][:, m, :], h_raw[:, m % 2, :], 3 * KH * t + (1 + layer) * KH + m)
                    if layer == 0 and more:
                        split_y(t + 1)
                dve.wait_ge(s["resid2_loaded"], 16 * (t + 1))
                if not is_first(t):
                    dve.wait_ge(s["out_stored"], HEAD + 16 * t)
                for m in range(KD):
                    dve.wait_ge(s["c_mm"], C_UNITS * t + 4 * KH + m + 1)
                    nc.vector.scalar_tensor_tensor(out=outs[:, m, :], in0=banks[6 + m][:, :], scalar=SC_W3[:, m:m + 1], in1=resid2[:, m, :],
                                                   op0=ALU.mult, op1=ALU.add).then_inc(s["out_ready"], 1)

            with dve.Fori(0, TILES - 1) as t:
                ffn_tile(t, True)
            ffn_tile(TILES - 1, False)

        @block.tensor
        def _(pe):
            mm = nc.tensor.matmul

            def half_rows(par):
                return slice(SLOT * par, SLOT * (par + 1))

            def adapter_in(n, tail):
                pe.wait_ge(s["front_loaded"], 80 * (n + 1))
                if not is_first(n):
                    pe.wait_ge(s["keys_out"], n)
                    if tail:
                        pe.wait_ge(s["x1_out"], HEAD + KD * (n - 3))
                for k in range(KD):
                    last = mm(side[0][0:A, 0:T], w1c[:, k, :], xt[:, k, :], start=k == 0, stop=k == KD - 1)
                last.then_inc(s["hidden_mm"], 1)

            def adapter_out(n):
                pe.wait_ge(s["hidden_out"], n + 1)
                if not is_first(n):
                    pe.wait_ge(s["qv_out"], NT * (n - 1) + 1)
                for t in range(NT):
                    last = mm(side[1][:, t * D:(t + 1) * D], h_t[:, t * P:(t + 1) * P], w2c[:, :], start=True, stop=True)
                last.then_inc(s["adapted_mm"], 1)

            def norm_transposed(n, tail):
                pe.wait_ge(s["norm_ready"], NT * (n + 1))
                if tail:
                    pe.wait_ge(s["att_out"], NT * (n - 3) + 1)
                for k in range(KD):
                    for t in range(NT):
                        last = nc.tensor.transpose(side[0][:, k * T + t * P:k * T + (t + 1) * P], norm[:, t, k * P:(k + 1) * P], ident[:, :])
                last.then_inc(s["norm_t_mm"], 1)

            def project_keys(n):
                pe.wait_ge(s["norm_t_out"], n + 1)
                for k in range(KD):
                    last = mm(side[0][:, 0:T], wk[:, k, :], norm_t[:, k, :], start=k == 0, stop=k == KD - 1)
                last.then_inc(s["keys_mm"], 1)

            def project_queries(n, t, tail):
                if t == 0:
                    if tail:
                        pe.wait_ge(s["att_t_out"], n - 2)
                elif not is_first(n):
                    pe.wait_ge(s["max_out"], UNITS * n)
                dst = max_bank[0] if t else side[1]
                for k in range(KD):
                    last = mm(dst[:, 0:D + HD], norm_t[:, k, t * P:(t + 1) * P], wqv[:, k, :], start=k == 0, stop=k == KD - 1)
                last.then_inc(s["qv_mm"], 1)

            def queries_transposed(n, t, j, tail):
                if j == 0:
                    pe.wait_ge(s["q_low"], NT * n + t + 1)
                    pe.wait_ge(s["q_again"], NT * n + t + 1)
                if tail and (t, j) == (0, 1):
                    pe.wait_ge(s["early_out"], n - 1)
                elif tail and (t, j) == (1, 0):
                    pe.wait_ge(s["late_out"], n - 1)
                elif t == 1:
                    pe.wait_ge(s["q_t_out"], 4 * n + j + 1)
                for c in range(4):
                    pair = 4 * j + c
                    last = nc.tensor.transpose(ring[j][:, c * P:(c + 1) * P], q_parts[:, t, 2 * pair:2 * pair + 2, :], ident[:, :])
                last.then_inc(s["q_t_mm"], 1)

            def max_scores(n, odd, u):
                t, first, pairs = max_fill(u // 2)
                par = u % 2
                if par == 0:
                    pe.wait_ge(s["q_t_out"], 4 * n + 2 * t + first // 4 + 1)
                if u == 0:
                    pe.wait_ge(s["keys_moved"], n + 1)
                    pe.wait_ge(s["qv_out"], NT * (n + 1))
                elif u == 1 and not is_first(n):
                    pe.wait_ge(s["max_t_out"], n)
                elif u >= 2:
                    pe.wait_ge(s["max_out"], UNITS * n + u - 1)
                keys_seen = P * (t + 1)
                r = half_rows(par)
                for c in range(pairs):
                    mm(max_bank[par][:, c * keys_seen:(c + 1) * keys_seen], q_t[odd][r, first + c, t * P:(t + 1) * P], keys[odd][r, 0:keys_seen],
                       start=c == 0, stop=False)
                diag = max_bank[par][:, :].rearrange("p (h k) -> p h k", h=pairs)[:, :, keys_seen - P:keys_seen]
                mm(diag, ident_b[:, :], mask[:, 0:pairs, :], start=False, stop=True).then_inc(s["max_mm"], 1)

            def maxima_transposed(n):
                pe.wait_ge(s["m2_ready"], n + 1)
                for t in range(NT):
                    last = nc.tensor.transpose(max_bank[1][0:4 * NP, t * P:(t + 1) * P], m2[:, t].rearrange("p a i c -> p (a i c)"), ident[:, :])
                last.then_inc(s["max_t_mm"], 1)

            def scores(b, odd, u):
                if u == 0:
                    pe.wait_ge(s["maxima_moved"], 64 * (b + 1))
                if u >= 2 or not is_first(b):
                    pe.wait_ge(s["exp_done"], UNITS * b + u - 1)
                first, pairs, k0, q0 = score_fill(u // 2)
                par = u % 2
                r = half_rows(par)
                mm(score_bank[par][:, :].rearrange("p (c t) -> p c t", c=pairs), keys[odd][r, k0:k0 + P], q_t[odd][r, first:first + pairs, q0:T],
                   start=True, stop=True).then_inc(s["score_mm"], 1)

            def products(b, odd, late, maxima):
                pe.wait_ge(s["masked"], FILLS * b + (6 if late else 3))
                if late and maxima:
                    pe.wait_ge(s["q_t_out"], 4 * (b + 2) + 1)
                elif late:
                    pe.wait_ge(s["late_out"], b)
                elif maxima:
                    pe.wait_ge(s["q_t_out"], 4 * (b + 2))
                else:
                    pe.wait_ge(s["early_out"], b)
                if not late:
                    pe.wait_ge(s["values_moved"], b + 1)
                dst = ring[0 if late else 1]
                for g in (2, 3) if late else (0, 1):
                    at = (g % 2) * T
                    for key_tile in range(NT):
                        for j in range(4):
                            c, par = j // 2, j % 2
                            rows = slice(32 * j, 32 * (j + 1))
                            if key_tile == 0:
                                last = mm(dst[rows, at:at + T], values[odd][:, 0, :], p0[:, g, par, c, :], start=True, stop=False)
                            else:
                                last = mm(dst[rows, at + P:at + T], values[odd][:, 1, :], p1[:, g // 2, par, 2 * (g % 2) + c, :],
                                          start=False, stop=True)
                last.then_inc(s["late_mm" if late else "early_mm"], 1)

            def products_transposed(b, t, front):
                if t == 0:
                    pe.wait_ge(s["early_out"], b + 1)
                    pe.wait_ge(s["late_out"], b + 1)
                    if front:
                        pe.wait_ge(s["hidden_out"], b + 4)
                    else:
                        pe.wait_ge(s["x1_out"], HEAD + KD * b)
                elif front:
                    pe.wait_ge(s["u_out"], b + 4)
                else:
                    pe.wait_ge(s["qv_out"], NT * (B - 1) + 1)
                    pe.wait_ge(s["att_t_out"], b)
                for g in range(4):
                    last = nc.tensor.transpose(side[t][:, g * P:(g + 1) * P], pv[:, g, t * P:(t + 1) * P], ident[:, :])
                last.then_inc(s["pv_t_mm"], 1)

            def attention_transposed(b):
                pe.wait_ge(s["att_out"], NT * (b + 1))
                for k in range(KD):
                    for t in range(NT):
                        last = nc.tensor.transpose(side[1][:, k * T + t * P:k * T + (t + 1) * P], att[:, t, k * P:(k + 1) * P], ident[:, :])
                last.then_inc(s["att_t_mm"], 1)

            def project_out(b, front):
                pe.wait_ge(s["att_t_out"], b + 1)
                if front:
                    pe.wait_ge(s["keys_out"], b + 4)
                for m in range(KD):
                    for k in range(KD):
                        last = mm(side[0][:, m * T:(m + 1) * T], wf[:, k, m * P:(m + 1) * P], att_t[:, k, :], start=k == 0, stop=k == KD - 1)
                last.then_inc(s["proj_mm"], 1)

            def iteration(b, odd, front, maxima, softmax, tail):
                other = 1 - odd
                if maxima:
                    queries_transposed(b + 1, 0, 0, tail)
                    queries_transposed(b + 1, 0, 1, tail)
                if front:
                    adapter_in(b + 2, tail)
                if maxima:
                    max_scores(b + 1, other, 0)
                    max_scores(b + 1, other, 1)
                if front:
                    adapter_out(b + 2)
                if tail:
                    products(b - 1, other, True, maxima)
                if softmax:
                    scores(b, odd, 0)
                if maxima:
                    max_scores(b + 1, other, 2)
                if softmax:
                    scores(b, odd, 1)
                if maxima:
                    max_scores(b + 1, other, 3)
                if softmax:
                    scores(b, odd, 2)
                    scores(b, odd, 3)
                if maxima:
                    queries_transposed(b + 1, 1, 0, tail)
                    queries_transposed(b + 1, 1, 1, tail)
                if softmax:
                    scores(b, odd, 4)
                if tail:
                    products_transposed(b - 1, 0, front)
                if maxima:
                    max_scores(b + 1, other, 4)
                if softmax:
                    scores(b, odd, 5)
                if tail:
                    products_transposed(b - 1, 1, front)
                if maxima:
                    max_scores(b + 1, other, 5)
                if softmax:
                    scores(b, odd, 6)
                if maxima:
                    max_scores(b + 1, other, 6)
                if softmax:
                    scores(b, odd, 7)
                    products(b, odd, False, maxima)
                if maxima:
                    max_scores(b + 1, other, 7)
                if front:
                    norm_transposed(b + 2, tail)
                if tail:
                    attention_transposed(b - 1)
                if maxima:
                    max_scores(b + 1, other, 8)
                if softmax:
                    scores(b, odd, 8)
                if maxima:
                    max_scores(b + 1, other, 9)
                if front:
                    project_keys(b + 2)
                if softmax:
                    scores(b, odd, 9)
                if maxima:
                    max_scores(b + 1, other, 10)
                    max_scores(b + 1, other, 11)
                if front:
                    project_queries(b + 2, 0, tail)
                if tail:
                    project_out(b - 1, front)
                if softmax:
                    scores(b, odd, 10)
                    scores(b, odd, 11)
                if maxima:
                    maxima_transposed(b + 1)
                if front:
                    project_queries(b + 2, 1, tail)

            pe.wait_ge(s["row_made"], 1)
            adapter_in(0, False)
            adapter_out(0)
            pe.wait_ge(s["const_loaded"], 112)
            pe.wait_ge(s["const_made"], 5)
            pe.wait_ge(s["ident_made"], 1)
            norm_transposed(0, False)
            project_keys(0)
            project_queries(0, 0, False)
            project_queries(0, 1, False)
            all_iterations(pe, iteration)
            products(B - 1, 1, True, False)
            products_transposed(B - 1, 0, False)
            products_transposed(B - 1, 1, False)
            attention_transposed(B - 1)
            project_out(B - 1, False)
            pe.wait_ge(s["late_mm"], B)
            pe.wait_ge(s["proj_mm"], B)
            pe.sem_inc(s["phase1_over"], 1)

            with pe.Fori(0, TILES) as t:
                pe.wait_ge(s["xa_split"], HEAD + t + 1)
                for m in range(KH):
                    if m == 2:
                        pe.wait_ge(s["x1_out"], HEAD + KD * B)
                    elif m >= 6:
                        pe.wait_ge(s["raw_ready"], KH * t + m - 5)
                    cols = slice(m * P, (m + 1) * P)
                    passes = [(w, v, k) for w, v in ((fc1_hi, xa_hi), (fc1_hi, xa_lo), (fc1_lo, xa_hi)) for k in range(KD)]
                    for i, (w, v, k) in enumerate(passes):
                        last = mm(banks[m % 6][:, :], w[:, k, cols], v[:, k, :], start=i == 0, stop=i == len(passes) - 1)
                    last.then_inc(s["unit_mm"], 1)
                pe.wait_ge(s["y_ready"], HEAD + (1 + BT) * t)
                pe.wait_ge(s["fc2_split"], 1)
                for k in range(KH):
                    pe.wait_ge(s["act_ready"], HEAD + KH * t + k + 1)
                    for i, (w, v) in enumerate(((fc2a_hi, g_hi), (fc2a_hi, g_lo), (fc2a_lo, g_hi))):
                        last = mm(banks[6][:, :], w[:, k, :], v[:, k, :], start=k == 0 and i == 0, stop=k == KH - 1 and i == 2)
                last.then_inc(s["unit_mm"], 1)
                pe.wait_ge(s["expert_split"], HEAD + BT * (t + 1))
                pe.wait_ge(s["fc2_split"], 1 + BT)
                for j in range(BT):
                    for k in range(KH):
                        for i, (w, v) in enumerate(((fc2b_hi, g_hi), (fc2b_hi, g_lo), (fc2b_lo, g_hi))):
                            last = mm(banks[7][:, j * T:(j + 1) * T], w[:, k, j, :], v[:, k, j * T:(j + 1) * T],
                                      start=k == 0 and i == 0, stop=k == KH - 1 and i == 2)
                last.then_inc(s["unit_mm"], 1)
            pe.wait_ge(s["bits_max"], 1)
            mm(banks[2][0:1, 0:1], low_bits[:, :], ones[:, :], start=True, stop=True).then_inc(s["bits_summed"], 1)
            pe.wait_ge(s["flag_ready"], 1)
            pe.sem_inc(s["phase2_over"], 1)

            def ffn(dt):
                def w_at(at, k, width, m):
                    w = ffn_w[:, at + k * width + m * P:at + k * width + (m + 1) * P]
                    return w if dt is F32R else w.bitcast(dt)

                def v_at(v, k):
                    return v[:, k, :] if dt is F32R else v[:, k, :].bitcast(dt)

                def part(bank, at, width, m, hi, lo, tiles, k, ready):
                    if ready is not None and m == 0:
                        pe.wait_ge(s["c_ready"], ready + k + 1)
                    for i, v in enumerate((hi, lo)):
                        last = mm(bank, w_at(at, k, width, m), v_at(v, k), start=k == 0 and i == 0, stop=k == tiles - 1 and i == 1)
                    if k == tiles - 1:
                        last.then_inc(s["c_mm"], 1)

                def unit(bank, at, width, m, hi, lo, tiles, ready):
                    for k in range(tiles):
                        part(bank, at, width, m, hi, lo, tiles, k, ready)

                with pe.Fori(0, TILES) as t:
                    pe.wait_ge(s["yc_split"], HEAD + t + 1)
                    for m in range(KH):
                        if m >= 4:
                            pe.wait_ge(s["sil_ready"], KH * t + m - 3)
                        elif m == 3:
                            pe.wait_ge(s["y_ready"], HEAD + (1 + BT) * TILES)
                            pe.wait_ge(s["out_ready"], HEAD + KD * t)
                        unit(banks[(2 * m) % 8][:, :], W1_AT, HID, m, yc_hi, yc_lo, KD, None)
                        if m >= 4:
                            pe.wait_ge(s["prod_ready"], HEAD + KH * t + m - 3)
                        unit(banks[(2 * m + 1) % 8][:, :], W2_AT, HID, m, yc_hi, yc_lo, KD, None)
                    early_parts = [(m, k) for m in range(2) for k in range(KH - 1)] + [(m, KH - 1) for m in range(2)]
                    for m, k in early_parts:
                        if k == 0:
                            pe.wait_ge(s["prod_ready"], HEAD + KH * t + 5)
                        part(banks[m][:, :], H1_AT, HID, m, h_hi[0], h_lo[0], KH, k, 3 * KH * t)
                    for layer, at in enumerate((H1_AT, H2_AT)):
                        for m in range(0 if layer else 2, KH):
                            if layer == 0:
                                pe.wait_ge(s["prod_ready"], HEAD + KH * t + 5 + m // 2)
                            else:
                                pe.wait_ge(s["c_act"], HEAD + 2 * KH * t + m + 1)
                            unit(banks[m][:, :], at, HID, m, h_hi[layer], h_lo[layer], KH, 3 * KH * t + layer * KH)
                    for m in range(KD):
                        pe.wait_ge(s["c_act"], HEAD + 2 * KH * t + KH + 6 + m + 1)
                        unit(banks[6 + m][:, :], W3_AT, D, m, h_hi[0], h_lo[0], KH, 3 * KH * t + 2 * KH)

            with pe.register("low_bits_found") as found:
                nc.tensor.reg_load(found, low_count[0:1, 0:1])
                with pe.If_ne(found, 0):
                    ffn(F32)
                with pe.Else():
                    ffn(F32R)


def tiles(a):
    a = np.ascontiguousarray(a)
    return np.ascontiguousarray(a.reshape(-1, P, a.shape[-1]).transpose(1, 0, 2))


def kernel(**inputs):
    import ml_dtypes
    import concourse.bacc as _bacc
    from concourse.bass_utils import run_bass_kernel_spmd as _run

    g = {k: np.asarray(v) for k, v in inputs.items()}
    z = np.zeros
    x = g["x"]
    a = {}
    a["x_t"] = tiles(x.reshape(TOK, D).T)
    a["x_tok"] = x.reshape(B, NT, P, D).transpose(0, 2, 1, 3)
    a["lang"] = g["itok_B_0_8"].reshape(1, B)
    a["expert"] = g["itok_B_0_15"].reshape(1, B)
    a["cond_w1"] = g["L0_cond_W1"].reshape(L, KD, P, A).transpose(0, 2, 1, 3)
    a["cond_w2"] = np.concatenate([g["L0_cond_W2"], g["L0_cond_b2"][:, None, :]], 1)
    vec = z((L, P, 5), np.float32)
    vec[:, :, 0:2] = g["L0_cond_gamma"].reshape(L, KD, P).transpose(0, 2, 1)
    vec[:, :, 2:4] = g["L0_cond_beta"].reshape(L, KD, P).transpose(0, 2, 1)
    vec[:, 0:A, 4] = g["L0_cond_b1"]
    a["cond_vec"] = vec
    a["w_qv"] = tiles(np.concatenate([g["L0_attn_Wq"].T, g["L0_attn_Wv"].T], 1))
    wk = z((D, P), np.float32)
    for at in (0, 16, 32, 64, 80, 96):
        wk[:, at:at + HD] = g["L0_attn_Wk"].T
    a["w_k"] = tiles(wk)
    a["w_f"] = tiles(g["L0_attn_Wf"].T)
    a["b_f"] = g["L0_attn_bf"].reshape(KD, P).T
    a["ident_d"] = np.eye(P, dtype=np.float32)
    q, k = np.arange(P)[:, None, None], np.arange(P)[None, None, :]
    a["mask_d"] = np.broadcast_to(np.where(k > q, -1e30, 0.0), (P, 4, P)).astype(ml_dtypes.bfloat16)
    key_row = z((P, 1), np.float32)
    for par in range(2):
        key_row[SLOT * par + MAX_ROW:SLOT * par + MAX_ROW + 2] = -1.0
    a["key_row_d"] = key_row
    a["fc1_w"] = tiles(g["L0_cond2_fc1_w"].T)
    a["fc1_b"] = g["L0_cond2_fc1_b"].reshape(KH, P).T
    a["fc2_w"] = tiles(g["L0_cond2_fc2_w"].T)
    fc2_b = z((2, P, 1), np.float32)
    fc2_b.reshape(-1)[0:SHARED] = g["L0_cond2_fc2_b"]
    a["fc2_b"] = fc2_b
    a["exp_w"] = g["L0_cond2_experts_w"].reshape(E, PART, KH, P).transpose(0, 3, 2, 1)
    a["exp_b"] = g["L0_cond2_experts_b"].reshape(E, PART, 1)
    a["ffn_d"] = np.concatenate([tiles(g[f"L0_ffn_{n}_w"].T).reshape(P, -1) for n in ("w1", "w2", "h1", "h2", "w3")], 1)
    a["ffn_s"] = np.concatenate([g[f"L0_ffn_{n}_s"].reshape(-1, P).T for n in ("w1", "w2", "h1", "h2", "w3")], 1)

    nc = _bacc.Bacc("TRN2", target_bir_lowering=False, num_devices=1)
    arrays, args = {}, {}
    for name, v in a.items():
        v = np.ascontiguousarray(v)
        arrays[f"in_{name}"] = v
        args[name] = nc.dram_tensor(f"in_{name}", v.shape, mybir.dt.from_np(v.dtype), kind="ExternalInput").ap()
    out_t = nc.dram_tensor("out_t", (P, KD, TOK), F32, kind="ExternalOutput").ap()
    build(nc, out_t=out_t, **args)
    r = _run(nc, [arrays], core_ids=[0])
    got = r.results[0]["out_t"]
    return np.ascontiguousarray(got.transpose(1, 0, 2).reshape(D, TOK).T.reshape(B, T, D))
```
